# Optimizing a Trainium2 kernel written in Bass

```python
import numpy as np
import jax
import jax.numpy as jnp

def _softmax(x, axis=-1):
    return jax.nn.softmax(x, axis=axis)

def _gelu(x):
    return jax.nn.gelu(x, approximate=True)

def _silu(x):
    return jax.nn.silu(x)

def _sigmoid(x):
    return jax.nn.sigmoid(x)

def _layernorm(x, axis=-1, eps=1e-05):
    m = jnp.mean(x, axis=axis, keepdims=True)
    v = jnp.var(x, axis=axis, keepdims=True)
    return (x - m) / jnp.sqrt(v + eps)

def _scatter_add(tgt, idx, src, axis=0):
    return tgt.at[idx].add(src)

def _segment_sum(src, seg, n):
    return jax.ops.segment_sum(src, seg, n)
kernel_name = 'mk_rec_standalone_d1_rec_r8_3181fa'

def setup_inputs(seed: int=0):
    np.random.seed(seed)
    _w = jnp.asarray

    def _rec_inputs():
        import jax
        import jax.numpy as jnp
        _rk = jax.random.key(seed)
        r_dense = -0.00338568 + 1.0005 * jax.random.normal(jax.random.fold_in(_rk, 1), (512, 13), jnp.float32)
        r_sparse = jnp.stack([jax.random.randint(jax.random.fold_in(jax.random.fold_in(_rk, 2), 0), (512,), 2, 12500, jnp.int32), jax.random.randint(jax.random.fold_in(jax.random.fold_in(_rk, 2), 1), (512,), 1, 99999, jnp.int32), jax.random.randint(jax.random.fold_in(jax.random.fold_in(_rk, 2), 2), (512,), 0, 12500, jnp.int32), jax.random.randint(jax.random.fold_in(jax.random.fold_in(_rk, 2), 3), (512,), 5, 12500, jnp.int32), jax.random.randint(jax.random.fold_in(jax.random.fold_in(_rk, 2), 4), (512,), 20, 99993, jnp.int32), jax.random.randint(jax.random.fold_in(jax.random.fold_in(_rk, 2), 5), (512,), 0, 99993, jnp.int32), jax.random.randint(jax.random.fold_in(jax.random.fold_in(_rk, 2), 6), (512,), 2, 99999, jnp.int32), jax.random.randint(jax.random.fold_in(jax.random.fold_in(_rk, 2), 7), (512,), 2, 99995, jnp.int32), jax.random.randint(jax.random.fold_in(jax.random.fold_in(_rk, 2), 8), (512,), 0, 99999, jnp.int32), jax.random.randint(jax.random.fold_in(jax.random.fold_in(_rk, 2), 9), (512,), 2, 99986, jnp.int32), jax.random.randint(jax.random.fold_in(jax.random.fold_in(_rk, 2), 10), (512,), 4, 99999, jnp.int32), jax.random.randint(jax.random.fold_in(jax.random.fold_in(_rk, 2), 11), (512,), 15, 99999, jnp.int32), jax.random.randint(jax.random.fold_in(jax.random.fold_in(_rk, 2), 12), (512,), 0, 99989, jnp.int32), jax.random.randint(jax.random.fold_in(jax.random.fold_in(_rk, 2), 13), (512,), 5, 99990, jnp.int32), jax.random.randint(jax.random.fold_in(jax.random.fold_in(_rk, 2), 14), (512,), 2, 99996, jnp.int32), jax.random.randint(jax.random.fold_in(jax.random.fold_in(_rk, 2), 15), (512,), 3, 99994, jnp.int32), jax.random.randint(jax.random.fold_in(jax.random.fold_in(_rk, 2), 16), (512,), 0, 99998, jnp.int32), jax.random.randint(jax.random.fold_in(jax.random.fold_in(_rk, 2), 17), (512,), 13, 99998, jnp.int32), jax.random.randint(jax.random.fold_in(jax.random.fold_in(_rk, 2), 18), (512,), 10, 12498, jnp.int32), jax.random.randint(jax.random.fold_in(jax.random.fold_in(_rk, 2), 19), (512,), 0, 99999, jnp.int32), jax.random.randint(jax.random.fold_in(jax.random.fold_in(_rk, 2), 20), (512,), 0, 99995, jnp.int32), jax.random.randint(jax.random.fold_in(jax.random.fold_in(_rk, 2), 21), (512,), 1, 99998, jnp.int32), jax.random.randint(jax.random.fold_in(jax.random.fold_in(_rk, 2), 22), (512,), 1, 99997, jnp.int32), jax.random.randint(jax.random.fold_in(jax.random.fold_in(_rk, 2), 23), (512,), 2, 99989, jnp.int32), jax.random.randint(jax.random.fold_in(jax.random.fold_in(_rk, 2), 24), (512,), 6, 12500, jnp.int32), jax.random.randint(jax.random.fold_in(jax.random.fold_in(_rk, 2), 25), (512,), 2, 99995, jnp.int32)], axis=1)
        return (r_dense, r_sparse)
    r_dense, r_sparse = _rec_inputs()

    def _L0_rec_setup():
        import jax, jax.numpy as jnp
        import numpy as np
        B = 2048
        NUM_DENSE = 13
        NUM_SPARSE = 26
        VOCAB = 12500
        DIM = 128
        BOTTOM = [512, 256, 128]
        TOP = [1024, 1024, 512, 256, 1]
        NUM_FEAT = 1 + NUM_SPARSE
        _TRIU = np.triu_indices(NUM_FEAT, k=1)

        def _linear_params(key, dims):
            Ws, bs = ([], [])
            for i, (din, dout) in enumerate(zip(dims[:-1], dims[1:])):
                k = jax.random.fold_in(key, i)
                Ws.append(jax.random.normal(k, (din, dout), dtype=jnp.float32) * (1.0 / np.sqrt(din)))
                bs.append(jnp.zeros((dout,), dtype=jnp.float32))
            return (Ws, bs)

        def _mlp(x, Ws, bs):
            for W, b in zip(Ws, bs):
                x = jax.nn.relu(x @ W + b)
            return x
        key = jax.random.key(seed)
        k_dense, k_sparse, k_emb, k_bot, k_top = jax.random.split(key, 5)
        dense = jax.random.normal(k_dense, (B, NUM_DENSE), dtype=jnp.float32)
        sparse = jax.random.randint(k_sparse, (B, NUM_SPARSE), 0, VOCAB, dtype=jnp.int64)
        emb_tables = jax.random.normal(k_emb, (NUM_SPARSE, VOCAB, DIM), dtype=jnp.float32) * 0.01
        bWs, bbs = _linear_params(k_bot, [NUM_DENSE] + BOTTOM)
        inter_dim = NUM_FEAT * (NUM_FEAT - 1) // 2 + BOTTOM[-1]
        tWs, tbs = _linear_params(k_top, [inter_dim] + TOP)
        return {'dense': dense, 'sparse': sparse, 'emb_tables': emb_tables, 'bw0': bWs[0], 'bb0': bbs[0], 'bw1': bWs[1], 'bb1': bbs[1], 'bw2': bWs[2], 'bb2': bbs[2], 'tw0': tWs[0], 'tb0': tbs[0], 'tw1': tWs[1], 'tb1': tbs[1], 'tw2': tWs[2], 'tb2': tbs[2], 'tw3': tWs[3], 'tb3': tbs[3], 'tw4': tWs[4], 'tb4': tbs[4]}
    _L0_rec_all = _L0_rec_setup()
    _L0_rec_in = {k: v for k, v in _L0_rec_all.items() if k in ('emb_tables', 'bw0', 'bb0', 'bw1', 'bb1', 'bw2', 'bb2', 'tw0', 'tb0', 'tw1', 'tb1', 'tw2', 'tb2', 'tw3', 'tb3', 'tw4', 'tb4')}
    del _L0_rec_all
    return {'r_dense': r_dense, 'r_sparse': r_sparse, 'L0_rec_emb_tables': _L0_rec_in['emb_tables'], 'L0_rec_bw0': _L0_rec_in['bw0'], 'L0_rec_bb0': _L0_rec_in['bb0'], 'L0_rec_bw1': _L0_rec_in['bw1'], 'L0_rec_bb1': _L0_rec_in['bb1'], 'L0_rec_bw2': _L0_rec_in['bw2'], 'L0_rec_bb2': _L0_rec_in['bb2'], 'L0_rec_tw0': _L0_rec_in['tw0'], 'L0_rec_tb0': _L0_rec_in['tb0'], 'L0_rec_tw1': _L0_rec_in['tw1'], 'L0_rec_tb1': _L0_rec_in['tb1'], 'L0_rec_tw2': _L0_rec_in['tw2'], 'L0_rec_tb2': _L0_rec_in['tb2'], 'L0_rec_tw3': _L0_rec_in['tw3'], 'L0_rec_tb3': _L0_rec_in['tb3'], 'L0_rec_tw4': _L0_rec_in['tw4'], 'L0_rec_tb4': _L0_rec_in['tb4']}

def reference(r_dense, r_sparse, L0_rec_emb_tables, L0_rec_bw0, L0_rec_bb0, L0_rec_bw1, L0_rec_bb1, L0_rec_bw2, L0_rec_bb2, L0_rec_tw0, L0_rec_tb0, L0_rec_tw1, L0_rec_tb1, L0_rec_tw2, L0_rec_tb2, L0_rec_tw3, L0_rec_tb3, L0_rec_tw4, L0_rec_tb4):
    import jax
    import jax.numpy as jnp

    def _L0_rec_ref(dense, sparse, emb_tables, bw0, bb0, bw1, bb1, bw2, bb2, tw0, tb0, tw1, tb1, tw2, tb2, tw3, tb3, tw4, tb4):
        import jax, jax.numpy as jnp
        import numpy as np
        B = 2048
        NUM_DENSE = 13
        NUM_SPARSE = 26
        VOCAB = 12500
        DIM = 128
        BOTTOM = [512, 256, 128]
        TOP = [1024, 1024, 512, 256, 1]
        NUM_FEAT = 1 + NUM_SPARSE
        _TRIU = np.triu_indices(NUM_FEAT, k=1)

        def _linear_params(key, dims):
            Ws, bs = ([], [])
            for i, (din, dout) in enumerate(zip(dims[:-1], dims[1:])):
                k = jax.random.fold_in(key, i)
                Ws.append(jax.random.normal(k, (din, dout), dtype=jnp.float32) * (1.0 / np.sqrt(din)))
                bs.append(jnp.zeros((dout,), dtype=jnp.float32))
            return (Ws, bs)

        def _mlp(x, Ws, bs):
            for W, b in zip(Ws, bs):
                x = jax.nn.relu(x @ W + b)
            return x
        dense_out = _mlp(dense, [bw0, bw1, bw2], [bb0, bb1, bb2])
        sparse_embeds = emb_tables[jnp.arange(NUM_SPARSE)[None, :], sparse]
        features = jnp.concatenate([dense_out[:, None, :], sparse_embeds], axis=1)
        inter = jnp.einsum('bnd,bmd->bnm', features, features)
        interacted = inter[:, _TRIU[0], _TRIU[1]]
        concat = jnp.concatenate([dense_out, interacted], axis=-1)
        out = _mlp(concat, [tw0, tw1, tw2, tw3, tw4], [tb0, tb1, tb2, tb3, tb4])
        return out.squeeze(-1)
    y = _L0_rec_ref(r_dense, r_sparse, L0_rec_emb_tables, L0_rec_bw0, L0_rec_bb0, L0_rec_bw1, L0_rec_bb1, L0_rec_bw2, L0_rec_bb2, L0_rec_tw0, L0_rec_tb0, L0_rec_tw1, L0_rec_tb1, L0_rec_tw2, L0_rec_tb2, L0_rec_tw3, L0_rec_tb3, L0_rec_tw4, L0_rec_tb4)
    return y

_drawn_inputs = setup_inputs


def setup_inputs(seed=0):
    import zlib

    import numpy as np

    out = dict(_drawn_inputs(seed))
    spreads = {'L0_rec_bb0': (0.0, 0.1),
     'L0_rec_bb1': (0.0, 0.1),
     'L0_rec_bb2': (0.0, 0.1),
     'L0_rec_tb0': (0.0, 0.1),
     'L0_rec_tb1': (0.0, 0.1),
     'L0_rec_tb2': (0.0, 0.1),
     'L0_rec_tb3': (0.0, 0.1)}
    factors = {}
    for name, (base, spread) in spreads.items():
        noise = np.random.default_rng([zlib.crc32(name.encode()), seed]).standard_normal(out[name].shape)
        drawn = base * np.exp(spread * noise) if base else spread * noise
        out[name] = jnp.asarray(drawn.astype(out[name].dtype))
    for name, factor in factors.items():
        out[name] = (out[name] * factor).astype(out[name].dtype)
    return out
```

```python
from contextlib import ExitStack

import numpy as np

import concourse.bass as bass
from concourse import mybir

P = 128
TILES = 4
NUM_SPARSE = 26
NUM_DENSE = 13
VOCAB = 12500
DIM = 128
NB = 8
BOTTOM = [512, 256, 128]
TOP = [1024, 1024, 512, 256, 1]
BANK = 512

F32 = mybir.dt.float32
F32R = mybir.dt.float32r
I32 = mybir.dt.int32
ALU = mybir.AluOpType
ACT = mybir.ActivationFunctionType

SLOTS = 32
HIGH = 15
SETS_T = 3
LOW_ROWS = [14, 11, 8, 5]
LOW_J = [12, 9, 6, 3]
LAST_SLOT, LAST_ROWS = 16, 2
NLOW = HIGH - 1

GROUPS = P // 4
GCHUNK = 8
CHUNKS = GROUPS // GCHUNK
GCOLS = 4 * NUM_SPARSE

RING = 24
RAW = 5
FJOBS = -(-NUM_SPARSE // 4)

C_BB0, C_BB1, C_BB2, C_TB0, C_TB1, C_TB2, C_TB3, C_TW4, C_TB4 = 0, 4, 6, 7, 15, 23, 27, 29, 31
NCOLS = 32

PIECES = 16
FIRST_PIECE = [0, 4, 12, 16]


def stages():
    order = []
    pieces = iter(range(PIECES))
    order += [("BT",), ("W", next(pieces)), ("B0", 0), ("B0", 1), ("W", next(pieces)), ("B0", 2), ("B0", 3),
              ("W", next(pieces)), ("B1", 0), ("B1", 1), ("W", next(pieces)), ("B2",)]
    for j in range(FJOBS):
        order += [("F", 0, j)] + [("W", p) for p in (next(pieces, None), next(pieces, None)) if p is not None]
    order += [("G", 0, c) for c in range(CHUNKS)] + [("X", 0), ("M", 0, 0, 0), ("M", 0, 0, 1)]
    for k in range(TILES):
        more = k + 1 < TILES
        f = [("F", k + 1, j) for j in range(FJOBS)] if more else []
        g = [("G", k + 1, c) for c in range(CHUNKS)] if more else []
        order += f[0:2] + [("A", k, 0, 0), ("A", k, 0, 1)] + f[2:3]
        order += [("M", k, 1, 0)] + f[3:5] + [("M", k, 1, 1)] + f[5:]
        order += g[:2] + [("A", k, 1, 0), ("A", k, 1, 1)] + g[2:] + [("M", k, 2, 0)]
        if more:
            order += [("X", k + 1), ("M", k + 1, 0, 0), ("M", k + 1, 0, 1)]
        order += [("A", k, 2, 0), ("M3", k), ("M4", k)]
    return order


ORDER = stages()
T_KINDS = ("F", "A", "M3", "M4")
T_JOB = {s: n for n, s in enumerate(s for s in ORDER if s[0] in T_KINDS)}
O_JOB = {s: n for n, s in enumerate(s for s in ORDER if s[0] == "M")}
Z_JOB = O_JOB
H_JOB = {s: n for n, s in enumerate(s for s in ORDER if s[0] == "A")}
S_JOB = {s: n for n, s in enumerate(s for s in ORDER if s[0] == "A" and s[2] < 2)}
T_STAGE = {n: s for s, n in T_JOB.items()}


def f_put(s):
    n = T_JOB[s]
    return n % 2, sum(T_STAGE[m][0] == "F" for m in range(n % 2, n + 1, 2))


def in_features(j):
    return range(4 * j, min(4 * j + 4, NUM_SPARSE))


def dlrm(nc, tables, sparse, dense, cols, bw0, bw1, bw2, tw0, tw1, tw2, tw3, out):
    with ExitStack() as ctx:
        def sb(name, shape, dt, where=None):
            return (where or ctx).enter_context(nc.sbuf_tensor(name, shape, dt))

        def sem(name):
            return ctx.enter_context(nc.semaphore(name))

        ident = sb("ident", [P, P], F32)
        vec = sb("vec", [P, NCOLS], F32)
        sp_idx = sb("sp_idx", [P, TILES * NUM_SPARSE], I32)
        base = sb("base", [P, TILES * NUM_SPARSE], I32)
        wrap = sb("wrap", [P, TILES * NUM_SPARSE], F32)
        rows = sb("rows", [P, TILES * NUM_SPARSE], I32)
        out_row = sb("out_row", [1, P * TILES], F32)
        h4 = sb("h4", [P, 2, P], F32)
        w3 = sb("w3", [P, 4, TOP[3]], F32)
        emb = sb("emb", [P, RING, DIM], F32)
        FT = sb("FT", [P, P, SLOTS], F32)
        D = sb("D", [P, BANK], F32)
        Dhi = sb("Dhi", [P, BANK], F32R)
        Dlo = sb("Dlo", [P, BANK], F32R)
        X = sb("X", [P, SETS_T, P], F32)
        Xhi = sb("Xhi", [P, SETS_T, P], F32R)
        Xlo = sb("Xlo", [P, SETS_T, P], F32R)
        low = sb("low", [NLOW, NLOW, P], F32)
        z2 = sb("z2", [P, BANK], F32)
        with ExitStack() as early:
            raw = sb("raw", [P, RAW, 1024], F32, early)
        z = sb("z", [P, 1024], F32)
        hhi = [sb(f"hhi{n}", [P, 8, P], F32R) for n in range(2)]
        hlo = [sb(f"hlo{n}", [P, 8, P], F32R) for n in range(2)]
        whi = [sb(f"whi{n}", [P, 4 * (1, 2)[n], 1024], F32R) for n in range(2)]
        wlo = [sb(f"wlo{n}", [P, 4 * (1, 2)[n], 1024], F32R) for n in range(2)]
        with ExitStack() as early:
            dn = sb("dn", [P, TILES, NUM_DENSE], F32, early)
            xT = sb("xT", [NUM_DENSE, BANK], F32, early)
            b0 = sb("b0", [NUM_DENSE, BOTTOM[0]], F32, early)
            b1 = sb("b1", [P, 4, BOTTOM[1]], F32, early)
            b2 = sb("b2", [P, 2, BOTTOM[2]], F32, early)
            g1 = sb("g1", [P, 4, BANK], F32, early)
            g2 = sb("g2", [P, 2, BANK], F32, early)
        whi.append(sb("whi2", [P, 4, 1024], F32R))
        wlo.append(sb("wlo2", [P, 4, 1024], F32R))

        psT = [ctx.enter_context(nc.psum_tensor(f"psT{n}", [P, BANK], F32)) for n in range(2)]
        psG = [ctx.enter_context(nc.psum_tensor(f"psG{n}", [P, 2, BANK], F32)) for n in range(2)]
        psO = [ctx.enter_context(nc.psum_tensor(f"psO{n}", [P, BANK], F32)) for n in range(2)]

        idx_loaded = sem("idx_loaded")
        dense_loaded = sem("dense_loaded")
        vec_loaded = sem("vec_loaded")
        bw_loaded = [sem(f"bw{n}_loaded") for n in range(3)]
        w3_loaded = sem("w3_loaded")
        raw_loaded = [sem(f"raw{n}_loaded") for n in range(RAW)]
        base_made = sem("base_made")
        ident_made = sem("ident_made")
        idx_step = sem("idx_step")
        pads_zero = sem("pads_zero")
        gathered = [sem(f"gathered{n}") for n in range(RING)]
        w_hi_made = sem("w_hi_made")
        w_lo_made = sem("w_lo_made")
        bottom_product = sem("bottom_product")
        bottom_out = sem("bottom_out")
        d_hi_made = sem("d_hi_made")
        d_split = sem("d_split")
        t_full = [sem(f"t_full{n}") for n in range(2)]
        t_put = [sem(f"t_put{n}") for n in range(2)]
        ft0_put = sem("ft0_put")
        g_full = sem("g_full")
        g_taken_dve = sem("g_taken_dve")
        g_taken_act = sem("g_taken_act")
        low_moved = sem("low_moved")
        x_hi_made = sem("x_hi_made")
        x_split = sem("x_split")
        o_full = [sem(f"o_full{n}") for n in range(2)]
        z_put = sem("z_put")
        h_put = sem("h_put")
        h_hi_made = sem("h_hi_made")
        h_split = sem("h_split")
        h4_put = sem("h4_put")
        row_put = sem("row_put")
        stored = sem("stored")

        w_src = [
            tw0.rearrange("(t p) n -> p t n", p=P),
            tw1.rearrange("(t p) n -> p t n", p=P),
            tw2.rearrange("(u v p) n -> p u v n", p=P, v=2),
        ]

        def piece(p):
            layer = 0 if p < 4 else 1 if p < 12 else 2
            return layer, p - FIRST_PIECE[layer]

        def t_wait_full(eng, s):
            n = T_JOB[s]
            eng.wait_ge(t_full[n % 2], n // 2 + 1)

        def o_wait_full(eng, s):
            n = O_JOB[s]
            eng.wait_ge(o_full[n % 2], n // 2 + 1)

        block = ctx.enter_context(nc.Block())

        @block.sync
        def _(sp):
            sp.dma_start(sp_idx[:, :], sparse.rearrange("(p k) f -> p (k f)", k=TILES)).then_inc(idx_loaded, 16)
            sp.dma_start(b0[:, :], bw0).then_inc(bw_loaded[0], 16)
            sp.dma_start(b1[:, :, :], bw1.rearrange("(t p) n -> p t n", p=P)).then_inc(bw_loaded[1], 16)
            sp.dma_start(b2[:, :, :], bw2.rearrange("(t p) n -> p t n", p=P)).then_inc(bw_loaded[2], 16)
            for p in range(PIECES):
                if p >= RAW:
                    sp.wait_ge(w_lo_made, p - RAW + 1)
                layer, t = piece(p)
                dst = raw[:, p % RAW, :]
                if layer == 2:
                    dst = dst.rearrange("p (v n) -> p v n", v=2)
                sp.dma_start(dst, w_src[layer][:, t]).then_inc(raw_loaded[p % RAW], 16)
            sp.dma_start(w3[:, :, :], tw3.rearrange("(t p) n -> p t n", p=P)).then_inc(w3_loaded, 16)
            for k in range(TILES):
                sp.wait_ge(g_taken_dve, CHUNKS * (k + 1))
                sp.wait_ge(g_taken_act, CHUNKS * (k + 1))
                for q in range(4):
                    r = LOW_ROWS[q]
                    sp.dma_start(X[32 * q + 32 - r:32 * q + 32, :, :],
                                 low[0:r, LOW_J[q] - 1:LOW_J[q] - 1 + SETS_T, :]).then_inc(low_moved, 16)
                sp.dma_start(X[LAST_SLOT:LAST_SLOT + LAST_ROWS, 0:2, :],
                             low[0:LAST_ROWS, 0:2, :]).then_inc(low_moved, 16)
            sp.wait_ge(row_put, TILES)
            sp.dma_start(out.rearrange("(a n) -> a n", a=1), out_row[:, :]).then_inc(stored, 16)
            sp.wait_ge(stored, 16)

        @block.gpsimd
        def _(pool):
            nc.gpsimd.iota(base[:, :], pattern=[[0, TILES], [VOCAB, NUM_SPARSE]], base=0,
                           channel_multiplier=0).then_inc(base_made, 1)
            nc.gpsimd.memset(ident[:, :], 0.0).then_inc(ident_made, 1)
            pool.wait_ge(ident_made, 1)
            nc.gpsimd.affine_select(out=ident[:, :], in_=ident[:, :], compare_op=ALU.not_equal, fill=1.0, base=0,
                                    pattern=[[-1, P]], channel_multiplier=1).then_inc(ident_made, 1)
            pool.wait_ge(idx_step, 4)
            for n in range(TILES * NUM_SPARSE):
                if n >= RING:
                    k, f = divmod(n - RING, NUM_SPARSE)
                    t_wait_full(pool, ("F", k, f // 4))
                nc.gpsimd.indirect_dma_start(
                    out=emb[:, n % RING, :], out_offset=None, in_=tables,
                    in_offset=bass.IndirectOffsetOnAxis(ap=rows[:, n:n + 1], axis=0),
                ).then_inc(gathered[n % RING], 16)

        @block.tensor
        def _(pe):
            def t_bank(s):
                n = T_JOB[s]
                if n >= 2:
                    before = T_STAGE[n - 2]
                    if before[0] == "F":
                        bank, count = f_put(before)
                        pe.wait_ge(t_put[bank], count)
                    elif before[0] == "A":
                        pe.wait_ge(h_put, H_JOB[before] + 1)
                    elif before[0] == "M3":
                        pe.wait_ge(h4_put, before[1] + 1)
                    else:
                        pe.wait_ge(row_put, before[1] + 1)
                return psT[n % 2], t_full[n % 2]

            def features(s):
                ps, full = t_bank(s)
                for a, f in enumerate(in_features(s[2])):
                    n = s[1] * NUM_SPARSE + f
                    pe.wait_ge(gathered[n % RING], 16 * (n // RING + 1))
                    last = nc.tensor.transpose(ps[:, P * a:P * a + P], emb[:, n % RING, :], ident[:, :])
                last.then_inc(full, 1)

            def gram(k, c):
                m = k * CHUNKS + c
                if c == 0:
                    for bank, count in sorted(dict(f_put(("F", k, j)) for j in range(FJOBS)).items()):
                        pe.wait_ge(t_put[bank], count)
                    pe.wait_ge(ft0_put, k + 1)
                if m >= 2:
                    pe.wait_ge(g_taken_dve, m - 1)
                    pe.wait_ge(g_taken_act, m - 1)
                for g in range(GCHUNK):
                    b = 4 * (GCHUNK * c + g)
                    last = nc.tensor.matmul(
                        psG[m % 2][:, g // 4, GCOLS * (g % 4):GCOLS * (g % 4) + GCOLS],
                        FT[:, b:b + 4, :], FT[:, b:b + 4, 1:1 + NUM_SPARSE], start=True, stop=True)
                last.then_inc(g_full, 1)

            def product(s):
                _, k, layer, n = s
                j = O_JOB[s]
                if j >= 2:
                    pe.wait_ge(z_put, j - 1)
                kt = (4, 8, 8)[layer]
                for t in range(kt):
                    if layer == 0:
                        hi, lo = ((Dhi[:, P * k:P * k + P], Dlo[:, P * k:P * k + P]) if t == 0 else
                                  (Xhi[:, t - 1, :], Xlo[:, t - 1, :]))
                        pe.wait_ge(*((d_split, 1) if t == 0 else (x_split, k + 1)))
                    else:
                        hi, lo = hhi[layer - 1][:, t, :], hlo[layer - 1][:, t, :]
                        if t % 4 == 0:
                            pe.wait_ge(h_split, S_JOB[("A", k, layer - 1, t // 4)] + 1)
                    if layer < 2:
                        w = [x[layer][:, t, BANK * n:BANK * n + BANK] for x in (whi, wlo)]
                        pe.wait_ge(w_lo_made, FIRST_PIECE[layer] + t + 1)
                    else:
                        w = [x[2][:, t // 2, BANK * (t % 2):BANK * (t % 2) + BANK] for x in (whi, wlo)]
                        pe.wait_ge(w_lo_made, FIRST_PIECE[2] + t // 2 + 1)
                    for i, (a, b) in enumerate(((hi, w[0]), (hi, w[1]), (lo, w[0]))):
                        last = nc.tensor.matmul(psO[j % 2][:, :], a, b, start=(t == 0 and i == 0),
                                                stop=(t == kt - 1 and i == 2))
                last.then_inc(o_full[j % 2], 1)

            def turn(s):
                _, k, layer, half = s
                pe.wait_ge(z_put, Z_JOB[("M", k, layer, half)] + 1)
                ps, full = t_bank(s)
                src = z2 if layer == 2 else z
                for a in range(4):
                    at = BANK * half + P * a
                    last = nc.tensor.transpose(ps[:, P * a:P * a + P], src[:, at:at + P], ident[:, :])
                last.then_inc(full, 1)

            for s in ORDER:
                if s[0] == "BT":
                    pe.wait_ge(ident_made, 2)
                    pe.wait_ge(dense_loaded, 16)
                    for k in range(TILES):
                        last = nc.tensor.transpose(psO[0][0:NUM_DENSE, P * k:P * k + P], dn[:, k, :], ident[:, :])
                    last.then_inc(bottom_product, 1)
                elif s[0] == "B0":
                    pe.wait_ge(bottom_out, 1)
                    pe.wait_ge(bw_loaded[0], 16)
                    nc.tensor.matmul(psG[s[1] // 2][:, s[1] % 2, :], b0[:, P * s[1]:P * s[1] + P], xT[:, :],
                                     start=True, stop=True).then_inc(bottom_product, 1)
                elif s[0] == "B1":
                    pe.wait_ge(bw_loaded[1], 16)
                    for t in range(4):
                        pe.wait_ge(bottom_out, 2 + t)
                        last = nc.tensor.matmul(psO[s[1]][:, :], b1[:, t, P * s[1]:P * s[1] + P], g1[:, t, :],
                                                start=(t == 0), stop=(t == 3))
                    last.then_inc(bottom_product, 1)
                elif s[0] == "B2":
                    pe.wait_ge(bw_loaded[2], 16)
                    for t in range(2):
                        pe.wait_ge(bottom_out, 6 + t)
                        last = nc.tensor.matmul(psG[0][:, 0, :], b2[:, t, :], g2[:, t, :],
                                                start=(t == 0), stop=(t == 1))
                    last.then_inc(bottom_product, 1)
                elif s[0] == "F":
                    features(s)
                elif s[0] == "G":
                    gram(s[1], s[2])
                elif s[0] == "M":
                    product(s)
                elif s[0] == "A":
                    turn(s)
                elif s[0] == "M3":
                    ps, full = t_bank(s)
                    pe.wait_ge(w3_loaded, 16)
                    pe.wait_ge(h_put, H_JOB[("A", s[1], 2, 0)] + 1)
                    for m in range(2):
                        for t in range(4):
                            last = nc.tensor.matmul(ps[:, P * m:P * m + P], w3[:, t, P * m:P * m + P],
                                                    z2[:, P * t:P * t + P], start=(t == 0), stop=(t == 3))
                    last.then_inc(full, 1)
                elif s[0] == "M4":
                    ps, full = t_bank(s)
                    pe.wait_ge(h4_put, s[1] + 1)
                    for t in range(2):
                        last = nc.tensor.matmul(ps[0:1, 0:P], vec[:, C_TW4 + t:C_TW4 + t + 1], h4[:, t, :],
                                                start=(t == 0), stop=(t == 1))
                    last.then_inc(full, 1)

        def put_features(copy, eng, s):
            t_wait_full(eng, s)
            n = T_JOB[s]
            fs = in_features(s[2])
            return copy(FT[:, :, 1 + fs[0]:1 + fs[0] + len(fs)],
                        psT[n % 2][:, 0:P * len(fs)].rearrange("p (f b) -> p b f", f=len(fs))).then_inc(t_put[n % 2], 1)

        def take_pairs(copy, eng, k, c, batches, taken):
            m = k * CHUNKS + c
            eng.wait_ge(g_full, m + 1)
            for b in batches:
                ps = psG[m % 2][:, :, 0:4 * GCOLS].rearrange("p u (g c j) -> p j u g c", g=4, c=4)[:, :, :, :, b]
                at = slice(4 * GCHUNK * c + b, 4 * GCHUNK * (c + 1), 4)
                dst = low[:, :, at].rearrange("p j (u g) -> p j u g", u=2)
                copy(dst, ps[32 * b:32 * b + NLOW, 0:NLOW])
                for q in range(4):
                    j = HIGH - 1 + SETS_T * q
                    dst = X[32 * q:32 * q + 32, :, at].rearrange("p j (u g) -> p j u g", u=2)
                    last = copy(dst, ps[32 * b:32 * b + 32, j:j + SETS_T])
            last.then_inc(taken, 1)

        @block.vector
        def _(dve):
            nc.vector.memset(FT[:, :, 1 + NUM_SPARSE:SLOTS], 0.0).then_inc(pads_zero, 1)
            dve.wait_ge(idx_loaded, 16)
            nc.vector.tensor_scalar(wrap[:, :], sp_idx[:, :], 0.0, float(VOCAB), ALU.is_lt,
                                    ALU.mult).then_inc(idx_step, 1)
            dve.wait_ge(idx_step, 1)
            nc.vector.tensor_tensor(wrap[:, :], wrap[:, :], sp_idx[:, :], ALU.add).then_inc(idx_step, 1)
            dve.wait_ge(idx_step, 2)
            nc.vector.tensor_scalar(wrap[:, :], wrap[:, :], 0.0, float(VOCAB - 1), ALU.max,
                                    ALU.min).then_inc(idx_step, 1)
            dve.wait_ge(idx_step, 3)
            dve.wait_ge(base_made, 1)
            nc.vector.tensor_tensor(rows[:, :], wrap[:, :], base[:, :], ALU.add).then_inc(idx_step, 1)

            for s in ORDER:
                if s[0] == "W":
                    layer, t = piece(s[1])
                    dve.wait_ge(w_hi_made, s[1] + 1)
                    if layer == 2:
                        dve.wait_ge(bottom_product, 8)
                    nc.vector.tensor_tensor(wlo[layer][:, t, :], raw[:, s[1] % RAW, :],
                                            whi[layer][:, t, :].bitcast(F32), ALU.subtract).then_inc(w_lo_made, 1)
                elif s[0] == "B2":
                    dve.wait_ge(bottom_out, 8)
                    nc.vector.tensor_copy(Dhi[:, :], D[:, :]).then_inc(d_hi_made, 1)
                    dve.wait_ge(d_hi_made, 1)
                    nc.vector.tensor_tensor(Dlo[:, :], D[:, :], Dhi[:, :].bitcast(F32), ALU.subtract).then_inc(d_split, 1)
                elif s[0] == "F":
                    if s[2] == 0:
                        t_wait_full(dve, s)
                        nc.vector.tensor_copy(FT[:, :, 0], D[:, P * s[1]:P * s[1] + P]).then_inc(ft0_put, 1)
                    if s[2] % 2 == 0:
                        put_features(nc.vector.tensor_copy, dve, s)
                elif s[0] == "G":
                    take_pairs(nc.vector.tensor_copy, dve, s[1], s[2], (0, 1), g_taken_dve)
                elif s[0] == "X":
                    dve.wait_ge(low_moved, 16 * 5 * (s[1] + 1))
                    dve.wait_ge(g_taken_act, CHUNKS * (s[1] + 1))
                    nc.vector.tensor_copy(Xhi[:, :, :], X[:, :, :]).then_inc(x_hi_made, 1)
                    dve.wait_ge(x_hi_made, s[1] + 1)
                    nc.vector.tensor_tensor(Xlo[:, :, :], X[:, :, :], Xhi[:, :, :].bitcast(F32),
                                            ALU.subtract).then_inc(x_split, 1)
                elif s[0] == "A" and s[2] < 2:
                    dve.wait_ge(h_put, H_JOB[s] + 1)
                    h = z[:, BANK * s[3]:BANK * s[3] + BANK].rearrange("p (a b) -> p a b", b=P)
                    hi, lo = (x[s[2]][:, 4 * s[3]:4 * s[3] + 4, :] for x in (hhi, hlo))
                    nc.vector.tensor_copy(hi, h).then_inc(h_hi_made, 1)
                    dve.wait_ge(h_hi_made, S_JOB[s] + 1)
                    nc.vector.tensor_tensor(lo, h, hi.bitcast(F32), ALU.subtract).then_inc(h_split, 1)

        @block.scalar
        def _(act):
            act.dma_start(dn[:, :, :], dense.rearrange("(p k) f -> p k f", k=TILES)).then_inc(dense_loaded, 16)
            act.dma_start(vec[:, :], cols).then_inc(vec_loaded, 16)
            made = [0]

            def relu(dst, src, col):
                return nc.scalar.activation(dst, src, ACT.Relu, bias=vec[0:dst.shape[0], col:col + 1])

            def bottom(dst, src, col):
                made[0] += 1
                act.wait_ge(bottom_product, made[0])
                last = (nc.scalar.copy(dst, src) if col is None else relu(dst, src, col))
                last.then_inc(bottom_out, 1)

            for s in ORDER:
                if s[0] == "W":
                    layer, t = piece(s[1])
                    act.wait_ge(raw_loaded[s[1] % RAW], 16 * (s[1] // RAW + 1))
                    if layer == 2:
                        act.wait_ge(bottom_product, 8)
                    nc.scalar.copy(whi[layer][:, t, :], raw[:, s[1] % RAW, :]).then_inc(w_hi_made, 1)
                elif s[0] == "BT":
                    bottom(xT[:, :], psO[0][0:NUM_DENSE, :], None)
                    act.wait_ge(vec_loaded, 16)
                elif s[0] == "B0":
                    bottom(g1[:, s[1], :], psG[s[1] // 2][:, s[1] % 2, :], C_BB0 + s[1])
                elif s[0] == "B1":
                    bottom(g2[:, s[1], :], psO[s[1]][:, :], C_BB1 + s[1])
                elif s[0] == "B2":
                    bottom(D[:, :], psG[0][:, 0, :], C_BB2)
                elif s[0] == "F" and s[2] % 2 == 1:
                    put_features(nc.scalar.copy, act, s)
                elif s[0] == "G":
                    if s[2] == 0 and s[1] > 0:
                        act.wait_ge(x_split, s[1])
                    take_pairs(nc.scalar.copy, act, s[1], s[2], (2, 3), g_taken_act)
                elif s[0] == "M":
                    _, k, layer, half = s
                    o_wait_full(act, s)
                    if layer == 2:
                        dst = z2[:, :]
                    else:
                        dst = z[:, BANK * half:BANK * half + BANK]
                        if (k, layer) == (0, 0):
                            act.wait_ge(w_lo_made, PIECES)
                        else:
                            before = (k, 0) if layer == 1 else (k - 1, 1)
                            act.wait_ge(h_split, S_JOB[("A", *before, half)] + 1)
                    nc.scalar.copy(dst, psO[O_JOB[s] % 2][:, :]).then_inc(z_put, 1)
                elif s[0] == "A":
                    _, k, layer, half = s
                    n = T_JOB[s]
                    t_wait_full(act, s)
                    dst = z2 if layer == 2 else z
                    col = (C_TB0, C_TB1, C_TB2)[layer] + 4 * half
                    for a in range(4):
                        at = BANK * half + P * a
                        last = relu(dst[:, at:at + P], psT[n % 2][:, P * a:P * a + P], col + a)
                    last.then_inc(h_put, 1)
                elif s[0] == "M3":
                    n = T_JOB[s]
                    t_wait_full(act, s)
                    for m in range(2):
                        last = relu(h4[:, m, :], psT[n % 2][:, P * m:P * m + P], C_TB3 + m)
                    last.then_inc(h4_put, 1)
                elif s[0] == "M4":
                    n = T_JOB[s]
                    t_wait_full(act, s)
                    relu(out_row[0:1, s[1]:P * TILES:TILES], psT[n % 2][0:1, 0:P], C_TB4).then_inc(row_put, 1)


_LAYOUT = ["tables", "sparse", "dense", "cols", "bw0", "bw1", "bw2", "tw0", "tw1", "tw2", "tw3"]


def row_order():
    first, total = BOTTOM[-1], BOTTOM[-1] + 351
    pair = {}
    for i in range(27):
        for j in range(i + 1, 27):
            pair[i, j] = first + len(pair)
    order = np.full(4 * P, total)
    order[:first] = np.arange(first)

    def place(t, slot, i, j):
        order[P * (1 + t) + slot] = pair.pop((i, j))

    for q in range(4):
        for t in range(SETS_T):
            for i in range(HIGH + SETS_T * q + t):
                place(t, 32 * q + i, i, HIGH + SETS_T * q + t)
            for i in range(LOW_J[q] + t):
                place(t, 32 * q + 32 - LOW_ROWS[q] + i, i, LOW_J[q] + t)
    for t in range(2):
        for i in range(1 + t):
            place(t, LAST_SLOT + i, i, 1 + t)
    assert not pair
    return order


def kernel(**inputs):
    import concourse.bacc as _bacc
    from concourse.bass_utils import run_bass_kernel_spmd as _run

    a = {n.replace("L0_rec_", ""): np.ascontiguousarray(x) for n, x in inputs.items()}

    def by_partition(x):
        return x.reshape(-1, P).T

    cols = np.zeros((P, NCOLS), np.float32)
    for name, at in (("bb0", C_BB0), ("bb1", C_BB1), ("bb2", C_BB2), ("tb0", C_TB0), ("tb1", C_TB1), ("tb2", C_TB2),
                     ("tb3", C_TB3), ("tw4", C_TW4)):
        x = by_partition(a[name])
        cols[:, at:at + x.shape[1]] = x
    cols[0, C_TB4] = a["tb4"][0]
    tw0 = np.concatenate([a["tw0"], np.zeros((1, TOP[0]), np.float32)])[row_order()]
    given = {
        "tables": a["emb_tables"].reshape(NUM_SPARSE * VOCAB, DIM), "sparse": a["r_sparse"], "dense": a["r_dense"],
        "cols": cols, "bw0": a["bw0"], "bw1": a["bw1"], "bw2": a["bw2"], "tw0": tw0, "tw1": a["tw1"],
        "tw2": a["tw2"], "tw3": a["tw3"],
    }
    nc = _bacc.Bacc("TRN2", target_bir_lowering=False, num_devices=1)
    args = [nc.dram_tensor(f"in_{n}", given[n].shape, mybir.dt.from_np(given[n].dtype), kind="ExternalInput").ap()
            for n in _LAYOUT]
    out = nc.dram_tensor("out", (P * TILES,), F32, kind="ExternalOutput").ap()
    dlrm(nc, *args, out)
    r = _run(nc, [{f"in_{n}": given[n] for n in _LAYOUT}], core_ids=[0])
    return r.results[0]["out"]
```

```python
from contextlib import ExitStack

import numpy as np

import concourse.bass as bass
from concourse import mybir

P = 128
TILES = 4
NUM_SPARSE = 26
NUM_DENSE = 13
VOCAB = 12500
DIM = 128
NB = 8
BOTTOM = [512, 256, 128]
TOP = [1024, 1024, 512, 256, 1]
BANK = 512

F32 = mybir.dt.float32
F32R = mybir.dt.float32r
I32 = mybir.dt.int32
ALU = mybir.AluOpType
ACT = mybir.ActivationFunctionType

FEATURES = 1 + NUM_SPARSE
SLOTS = 32
HIGH = 15
SETS_T = 3
LOW_ROWS = [14, 11, 8, 5]
LOW_J = [12, 9, 6, 3]
LAST_SLOT, LAST_ROWS = 16, 2
NLOW = HIGH - 1

GROUPS = P // 4
GCHUNK = 8
CHUNKS = GROUPS // GCHUNK
GROWS = 3 * SLOTS + FEATURES
GCOLS = 4 * NUM_SPARSE

PARTS = [1, 2, 2]
RING = 24
RAW = 5
FJOBS = -(-NUM_SPARSE // 4)

C_BB0, C_BB1, C_BB2, C_TB0, C_TB1, C_TB2, C_TB3, C_TW4, C_TB4 = 0, 4, 6, 7, 15, 23, 27, 29, 31
NCOLS = 32

PIECES = 16
FIRST_PIECE = [0, 4, 12, 16]


def stages():
    order = [("BT",), ("B0", 0), ("W", 0), ("B0", 1), ("W", 1), ("B0", 2), ("W", 2), ("B0", 3), ("W", 3),
             ("F", 0, 0), ("W", 4), ("W", 5), ("B1", 0), ("F", 0, 1), ("W", 6), ("W", 7), ("F", 0, 2), ("W", 8),
             ("W", 9), ("B1", 1), ("F", 0, 3), ("W", 10), ("F", 0, 4), ("B2",), ("W", 11), ("F", 0, 5), ("D", 0),
             ("F", 0, 6), ("W", 12), ("G", 0, 0), ("W", 13), ("G", 0, 1), ("G", 0, 2), ("G", 0, 3), ("F", 1, 0),
             ("F", 1, 1), ("W", 14), ("X", 0), ("W", 15)]
    for k in range(TILES):
        def m(layer, n, part=0):
            return ("M", k, layer, n, part)

        def a(layer, half):
            return ("A", k, layer, half)

        f = [("F", k + 1, j) for j in range(FJOBS)] + [("D", k + 1)]
        g = [("G", k + 1, c) for c in range(CHUNKS)]
        a2, m3, m4 = ("A", k - 1, 2, 0), ("M3", k - 1), ("M4", k - 1)
        if k == 0:
            order += [m(0, 0), f[2], a(0, 0), m(0, 1), a(0, 1), m(1, 0, 0), f[3], m(1, 0, 1), f[4],
                      a(1, 0), m(1, 1, 0), f[5], m(1, 1, 1), f[6], f[7], g[0], a(1, 1), g[1], g[2], g[3],
                      m(2, 0, 0), m(2, 0, 1), ("X", k + 1)]
        elif k + 1 < TILES:
            order += [m(0, 0), f[0], f[1], a(0, 0), m(0, 1), f[2], a2, a(0, 1), m(1, 0, 0), f[3], f[4], m(1, 0, 1),
                      f[5], f[6], f[7], m(1, 1, 0), a(1, 0), g[0], g[1], g[2], g[3], m(1, 1, 1), m3, a(1, 1),
                      m(2, 0, 0), m4, m(2, 0, 1), ("X", k + 1)]
        else:
            order += [m(0, 0), a2, a(0, 0), m(0, 1), m3, a(0, 1), m(1, 0, 0), m4, m(1, 0, 1), m(1, 1, 0), a(1, 0),
                      m(1, 1, 1), a(1, 1), m(2, 0, 0), m(2, 0, 1), a(2, 0), ("M3", k), ("M4", k)]
    return order


ORDER = stages()
T_KINDS = ("F", "A", "M3", "M4")
T_JOB = {s: n for n, s in enumerate(s for s in ORDER if s[0] in T_KINDS)}
O_JOB = {s[:4]: n for n, s in enumerate(s for s in ORDER if s[0] == "M" and s[4] == 0)}
H_JOB = {s: n for n, s in enumerate(s for s in ORDER if s[0] == "A")}
S_JOB = {s: n for n, s in enumerate(s for s in ORDER if s[0] == "A" and s[2] < 2)}
T_STAGE = {n: s for s, n in T_JOB.items()}


def f_put(s):
    n = T_JOB[s]
    return n % 2, sum(T_STAGE[m][0] == "F" for m in range(n % 2, n + 1, 2))


def in_features(j):
    return range(4 * j, min(4 * j + 4, NUM_SPARSE))


def dlrm(nc, tables, sparse, dense, cols, bw0, bw1, bw2, tw0, tw1, tw2, tw3, out):
    with ExitStack() as ctx:
        def sb(name, shape, dt, where=None):
            return (where or ctx).enter_context(nc.sbuf_tensor(name, shape, dt))

        def sem(name):
            return ctx.enter_context(nc.semaphore(name))

        ident = sb("ident", [P, P], F32)
        vec = sb("vec", [P, NCOLS], F32)
        sp_idx = sb("sp_idx", [P, TILES * NUM_SPARSE], I32)
        base = sb("base", [P, TILES * NUM_SPARSE], I32)
        wrap = sb("wrap", [P, TILES * NUM_SPARSE], F32)
        rows = sb("rows", [P, TILES * NUM_SPARSE], I32)
        out_row = sb("out_row", [1, P * TILES], F32)
        h4 = sb("h4", [P, 2, P], F32)
        w3 = sb("w3", [P, 4, TOP[3]], F32)
        emb = sb("emb", [P, RING, DIM], F32)
        FT = sb("FT", [P, P, SLOTS], F32)
        D = sb("D", [P, BANK], F32)
        Dhi = sb("Dhi", [P, BANK], F32R)
        Dlo = sb("Dlo", [P, BANK], F32R)
        X = sb("X", [P, SETS_T, P], F32)
        Xhi = sb("Xhi", [P, SETS_T, P], F32R)
        Xlo = sb("Xlo", [P, SETS_T, P], F32R)
        low = sb("low", [NLOW, NLOW, P], F32)
        z2 = sb("z2", [P, BANK], F32)
        with ExitStack() as early:
            raw = sb("raw", [P, RAW, 1024], F32, early)
        z = sb("z", [P, 1024], F32)
        hhi = [sb(f"hhi{n}", [P, 8, P], F32R) for n in range(2)]
        hlo = [sb(f"hlo{n}", [P, 8, P], F32R) for n in range(2)]
        whi = [sb(f"whi{n}", [P, 4 * (1, 2)[n], 1024], F32R) for n in range(2)]
        wlo = [sb(f"wlo{n}", [P, 4 * (1, 2)[n], 1024], F32R) for n in range(2)]
        with ExitStack() as early:
            dn = sb("dn", [P, TILES, NUM_DENSE], F32, early)
            xT = sb("xT", [NUM_DENSE, BANK], F32, early)
            b0 = sb("b0", [NUM_DENSE, BOTTOM[0]], F32, early)
            b1 = sb("b1", [P, 4, BOTTOM[1]], F32, early)
            b2 = sb("b2", [P, 2, BOTTOM[2]], F32, early)
            g1 = sb("g1", [P, 4, BANK], F32, early)
            g2 = sb("g2", [P, 2, BANK], F32, early)
        whi.append(sb("whi2", [P, 4, 1024], F32R))
        wlo.append(sb("wlo2", [P, 4, 1024], F32R))

        psT = [ctx.enter_context(nc.psum_tensor(f"psT{n}", [P, BANK], F32)) for n in range(2)]
        psG = [ctx.enter_context(nc.psum_tensor(f"psG{n}", [P, 2, BANK], F32)) for n in range(2)]
        psO = [ctx.enter_context(nc.psum_tensor(f"psO{n}", [P, BANK], F32)) for n in range(2)]

        idx_loaded = sem("idx_loaded")
        dense_loaded = sem("dense_loaded")
        vec_loaded = sem("vec_loaded")
        bw_loaded = [sem(f"bw{n}_loaded") for n in range(3)]
        w3_loaded = sem("w3_loaded")
        raw_loaded = [sem(f"raw{n}_loaded") for n in range(RAW)]
        base_made = sem("base_made")
        ident_made = sem("ident_made")
        idx_step = sem("idx_step")
        pads_zero = sem("pads_zero")
        gathered = [sem(f"gathered{n}") for n in range(RING)]
        w_hi_made = sem("w_hi_made")
        w_lo_made = sem("w_lo_made")
        bottom_product = sem("bottom_product")
        bottom_out = sem("bottom_out")
        d_hi_made = sem("d_hi_made")
        d_split = sem("d_split")
        t_full = [sem(f"t_full{n}") for n in range(2)]
        t_put = [sem(f"t_put{n}") for n in range(2)]
        ft0_put = sem("ft0_put")
        g_full = sem("g_full")
        low_taken_dve = sem("low_taken_dve")
        low_taken_act = sem("low_taken_act")
        g_taken_dve = sem("g_taken_dve")
        g_taken_act = sem("g_taken_act")
        low_moved = sem("low_moved")
        x_hi_made = sem("x_hi_made")
        x_split = sem("x_split")
        o_full = [sem(f"o_full{n}") for n in range(2)]
        z_put = sem("z_put")
        h_put = sem("h_put")
        h_hi_made = sem("h_hi_made")
        h_split = sem("h_split")
        h4_put = sem("h4_put")
        row_put = sem("row_put")
        stored = sem("stored")

        w_src = [
            tw0.rearrange("(t p) n -> p t n", p=P),
            tw1.rearrange("(t p) n -> p t n", p=P),
            tw2.rearrange("(u v p) n -> p u v n", p=P, v=2),
        ]

        def piece(p):
            layer = 0 if p < 4 else 1 if p < 12 else 2
            return layer, p - FIRST_PIECE[layer]

        def t_wait_full(eng, s):
            n = T_JOB[s]
            eng.wait_ge(t_full[n % 2], n // 2 + 1)

        def o_wait_full(eng, s):
            n = O_JOB[s[:4]]
            eng.wait_ge(o_full[n % 2], n // 2 + 1)

        block = ctx.enter_context(nc.Block())

        @block.sync
        def _(sp):
            sp.dma_start(sp_idx[:, :], sparse.rearrange("(p k) f -> p (k f)", k=TILES)).then_inc(idx_loaded, 16)
            sp.dma_start(b0[:, :], bw0).then_inc(bw_loaded[0], 16)
            sp.dma_start(b1[:, :, :], bw1.rearrange("(t p) n -> p t n", p=P)).then_inc(bw_loaded[1], 16)
            sp.dma_start(b2[:, :, :], bw2.rearrange("(t p) n -> p t n", p=P)).then_inc(bw_loaded[2], 16)
            for p in range(PIECES):
                if p >= RAW:
                    sp.wait_ge(w_lo_made, p - RAW + 1)
                layer, t = piece(p)
                if p == FIRST_PIECE[2]:
                    sp.wait_ge(gathered[NUM_SPARSE - 3], 16)
                dst = raw[:, p % RAW, :]
                if layer == 2:
                    dst = dst.rearrange("p (v n) -> p v n", v=2)
                sp.dma_start(dst, w_src[layer][:, t]).then_inc(raw_loaded[p % RAW], 16)
            sp.dma_start(w3[:, :, :], tw3.rearrange("(t p) n -> p t n", p=P)).then_inc(w3_loaded, 16)
            for k in range(TILES):
                sp.wait_ge(low_taken_dve, CHUNKS * (k + 1))
                sp.wait_ge(low_taken_act, CHUNKS * (k + 1))
                for q in range(4):
                    r = LOW_ROWS[q]
                    sp.dma_start(X[32 * q + 32 - r:32 * q + 32, :, :],
                                 low[0:r, LOW_J[q] - 1:LOW_J[q] - 1 + SETS_T, :]).then_inc(low_moved, 16)
                sp.wait_ge(g_taken_dve, CHUNKS * (k + 1))
                sp.wait_ge(g_taken_act, CHUNKS * (k + 1))
                sp.dma_start(X[LAST_SLOT:LAST_SLOT + LAST_ROWS, 0:2, :],
                             low[0:LAST_ROWS, 0:2, :]).then_inc(low_moved, 16)
            sp.wait_ge(row_put, TILES)
            sp.dma_start(out.rearrange("(a n) -> a n", a=1), out_row[:, :]).then_inc(stored, 16)
            sp.wait_ge(stored, 16)

        @block.gpsimd
        def _(pool):
            nc.gpsimd.iota(base[:, :], pattern=[[0, TILES], [VOCAB, NUM_SPARSE]], base=0,
                           channel_multiplier=0).then_inc(base_made, 1)
            nc.gpsimd.memset(ident[:, :], 0.0).then_inc(ident_made, 1)
            pool.wait_ge(ident_made, 1)
            nc.gpsimd.affine_select(out=ident[:, :], in_=ident[:, :], compare_op=ALU.not_equal, fill=1.0, base=0,
                                    pattern=[[-1, P]], channel_multiplier=1).then_inc(ident_made, 1)
            pool.wait_ge(idx_step, 4)
            for n in range(TILES * NUM_SPARSE):
                if n >= RING:
                    k, f = divmod(n - RING, NUM_SPARSE)
                    t_wait_full(pool, ("F", k, f // 4))
                nc.gpsimd.indirect_dma_start(
                    out=emb[:, n % RING, :], out_offset=None, in_=tables,
                    in_offset=bass.IndirectOffsetOnAxis(ap=rows[:, n:n + 1], axis=0),
                ).then_inc(gathered[n % RING], 16)

        @block.tensor
        def _(pe):
            def t_bank(s):
                n = T_JOB[s]
                if n >= 2:
                    before = T_STAGE[n - 2]
                    if before[0] == "F":
                        bank, count = f_put(before)
                        pe.wait_ge(t_put[bank], count)
                    elif before[0] == "A":
                        pe.wait_ge(h_put, 2 * (H_JOB[before] + 1))
                    elif before[0] == "M3":
                        pe.wait_ge(h4_put, before[1] + 1)
                    else:
                        pe.wait_ge(row_put, before[1] + 1)
                return psT[n % 2], t_full[n % 2]

            def features(s):
                ps, full = t_bank(s)
                for a, f in enumerate(in_features(s[2])):
                    n = s[1] * NUM_SPARSE + f
                    pe.wait_ge(gathered[n % RING], 16 * (n // RING + 1))
                    last = nc.tensor.transpose(ps[:, P * a:P * a + P], emb[:, n % RING, :], ident[:, :])
                last.then_inc(full, 1)

            def gram(k, c):
                m = k * CHUNKS + c
                if c == 0:
                    for bank, count in sorted(dict(f_put(("F", k, j)) for j in range(FJOBS)).items()):
                        pe.wait_ge(t_put[bank], count)
                    pe.wait_ge(ft0_put, k + 1)
                if m >= 2:
                    pe.wait_ge(g_taken_dve, m - 1)
                    pe.wait_ge(g_taken_act, m - 1)
                for g in range(GCHUNK):
                    b = 4 * (GCHUNK * c + g)
                    last = nc.tensor.matmul(
                        psG[m % 2][0:GROWS, g // 4, GCOLS * (g % 4):GCOLS * (g % 4) + GCOLS],
                        FT[:, b:b + 4, :].rearrange("p b f -> p (b f)")[:, 0:GROWS], FT[:, b:b + 4, 1:1 + NUM_SPARSE], start=True, stop=True)
                last.then_inc(g_full, 1)

            def product(s):
                _, k, layer, n, part = s
                j = O_JOB[s[:4]]
                if j >= 2 and part == 0:
                    pe.wait_ge(z_put, j - 1)
                kt = PARTS[layer] * 4
                for t in range(4 * part, 4 * part + 4):
                    if layer == 0:
                        hi, lo = ((Dhi[:, P * k:P * k + P], Dlo[:, P * k:P * k + P]) if t == 0 else
                                  (Xhi[:, t - 1, :], Xlo[:, t - 1, :]))
                        pe.wait_ge(*((d_split, 1) if t == 0 else (x_split, k + 1)))
                    else:
                        hi, lo = hhi[layer - 1][:, t, :], hlo[layer - 1][:, t, :]
                        if t % 4 == 0:
                            pe.wait_ge(h_split, S_JOB[("A", k, layer - 1, t // 4)] + 1)
                    if layer < 2:
                        w = [x[layer][:, t, BANK * n:BANK * n + BANK] for x in (whi, wlo)]
                        pe.wait_ge(w_lo_made, FIRST_PIECE[layer] + t + 1)
                    else:
                        w = [x[2][:, t // 2, BANK * (t % 2):BANK * (t % 2) + BANK] for x in (whi, wlo)]
                        pe.wait_ge(w_lo_made, FIRST_PIECE[2] + t // 2 + 1)
                    for i, (a, b) in enumerate(((hi, w[0]), (hi, w[1]), (lo, w[0]))):
                        last = nc.tensor.matmul(psO[j % 2][:, :], a, b, start=(t == 0 and i == 0),
                                                stop=(t == kt - 1 and i == 2))
                if t == kt - 1:
                    last.then_inc(o_full[j % 2], 1)

            def turn(s):
                _, k, layer, half = s
                pe.wait_ge(z_put, O_JOB["M", k, layer, half] + 1)
                ps, full = t_bank(s)
                src = z2 if layer == 2 else z
                for a in range(4):
                    at = BANK * half + P * a
                    last = nc.tensor.transpose(ps[:, P * a:P * a + P], src[:, at:at + P], ident[:, :])
                last.then_inc(full, 1)

            for s in ORDER:
                if s[0] == "BT":
                    pe.wait_ge(ident_made, 2)
                    pe.wait_ge(dense_loaded, 16)
                    for k in range(TILES):
                        last = nc.tensor.transpose(psO[0][0:NUM_DENSE, P * k:P * k + P], dn[:, k, :], ident[:, :])
                    last.then_inc(bottom_product, 1)
                elif s[0] == "B0":
                    pe.wait_ge(bottom_out, 1)
                    pe.wait_ge(bw_loaded[0], 16)
                    nc.tensor.matmul(psG[s[1] // 2][:, s[1] % 2, :], b0[:, P * s[1]:P * s[1] + P], xT[:, :],
                                     start=True, stop=True).then_inc(bottom_product, 1)
                elif s[0] == "B1":
                    pe.wait_ge(bw_loaded[1], 16)
                    for t in range(4):
                        pe.wait_ge(bottom_out, 2 + t)
                        last = nc.tensor.matmul(psO[s[1]][:, :], b1[:, t, P * s[1]:P * s[1] + P], g1[:, t, :],
                                                start=(t == 0), stop=(t == 3))
                    last.then_inc(bottom_product, 1)
                elif s[0] == "B2":
                    pe.wait_ge(bw_loaded[2], 16)
                    for t in range(2):
                        pe.wait_ge(bottom_out, 6 + t)
                        last = nc.tensor.matmul(psG[0][:, 0, :], b2[:, t, :], g2[:, t, :],
                                                start=(t == 0), stop=(t == 1))
                    last.then_inc(bottom_product, 1)
                elif s[0] == "F":
                    features(s)
                elif s[0] == "G":
                    gram(s[1], s[2])
                elif s[0] == "M":
                    product(s)
                elif s[0] == "A":
                    turn(s)
                elif s[0] == "M3":
                    ps, full = t_bank(s)
                    pe.wait_ge(w3_loaded, 16)
                    pe.wait_ge(h_put, 2 * (H_JOB["A", s[1], 2, 0] + 1))
                    for m in range(2):
                        for t in range(4):
                            last = nc.tensor.matmul(ps[:, P * m:P * m + P], w3[:, t, P * m:P * m + P],
                                                    z2[:, P * t:P * t + P], start=(t == 0), stop=(t == 3))
                    last.then_inc(full, 1)
                elif s[0] == "M4":
                    ps, full = t_bank(s)
                    pe.wait_ge(h4_put, s[1] + 1)
                    for t in range(2):
                        last = nc.tensor.matmul(ps[0:1, 0:P], vec[:, C_TW4 + t:C_TW4 + t + 1], h4[:, t, :],
                                                start=(t == 0), stop=(t == 1))
                    last.then_inc(full, 1)

        def put_features(copy, eng, s):
            t_wait_full(eng, s)
            n = T_JOB[s]
            fs = in_features(s[2])
            return copy(FT[:, :, 1 + fs[0]:1 + fs[0] + len(fs)],
                        psT[n % 2][:, 0:P * len(fs)].rearrange("p (f b) -> p b f", f=len(fs))).then_inc(t_put[n % 2], 1)

        def take_pairs(copy, eng, k, c, batches, taken):
            m = k * CHUNKS + c
            eng.wait_ge(g_full, m + 1)

            def pairs(b):
                return psG[m % 2][:, :, 0:4 * GCOLS].rearrange("p u (g c j) -> p j u g c", g=4, c=4)[:, :, :, :, b]

            def at(dst, b):
                return dst[:, :, 4 * GCHUNK * c + b:4 * GCHUNK * (c + 1):4].rearrange("p j (u g) -> p j u g", u=2)

            for b in batches:
                last = copy(at(low, b), pairs(b)[32 * b:32 * b + NLOW, 0:NLOW])
            last.then_inc(taken[0], 1)
            for b in batches:
                for q in range(4):
                    r, j = SLOTS - LOW_ROWS[q], HIGH - 1 + SETS_T * q
                    last = copy(at(X[32 * q:32 * q + r], b), pairs(b)[32 * b:32 * b + r, j:j + SETS_T])
            last.then_inc(taken[1], 1)

        @block.vector
        def _(dve):
            nc.vector.memset(FT[:, :, 1 + NUM_SPARSE:SLOTS], 0.0).then_inc(pads_zero, 1)
            dve.wait_ge(idx_loaded, 16)
            nc.vector.tensor_scalar(wrap[:, :], sp_idx[:, :], 0.0, float(VOCAB), ALU.is_lt,
                                    ALU.mult).then_inc(idx_step, 1)
            dve.wait_ge(idx_step, 1)
            nc.vector.tensor_tensor(wrap[:, :], wrap[:, :], sp_idx[:, :], ALU.add).then_inc(idx_step, 1)
            dve.wait_ge(idx_step, 2)
            nc.vector.tensor_scalar(wrap[:, :], wrap[:, :], 0.0, float(VOCAB - 1), ALU.max,
                                    ALU.min).then_inc(idx_step, 1)
            dve.wait_ge(idx_step, 3)
            dve.wait_ge(base_made, 1)
            nc.vector.tensor_tensor(rows[:, :], wrap[:, :], base[:, :], ALU.add).then_inc(idx_step, 1)

            dve.wait_ge(vec_loaded, 16)
            for s in ORDER:
                if s[0] == "W":
                    layer, t = piece(s[1])
                    dve.wait_ge(w_hi_made, s[1] + 1)
                    if layer == 2:
                        dve.wait_ge(bottom_product, 8)
                    nc.vector.tensor_tensor(wlo[layer][:, t, :], raw[:, s[1] % RAW, :],
                                            whi[layer][:, t, :].bitcast(F32), ALU.subtract).then_inc(w_lo_made, 1)
                elif s[0] == "B2":
                    dve.wait_ge(bottom_out, 8)
                    nc.vector.tensor_copy(Dhi[:, :], D[:, :]).then_inc(d_hi_made, 1)
                    dve.wait_ge(d_hi_made, 1)
                    nc.vector.tensor_tensor(Dlo[:, :], D[:, :], Dhi[:, :].bitcast(F32), ALU.subtract).then_inc(d_split, 1)
                elif s[0] == "F":
                    if s[2] % 2 == 0:
                        put_features(nc.vector.tensor_copy, dve, s)
                elif s[0] == "D":
                    nc.vector.tensor_copy(FT[:, :, 0], D[:, P * s[1]:P * s[1] + P]).then_inc(ft0_put, 1)
                elif s[0] == "G":
                    take_pairs(nc.vector.tensor_copy, dve, s[1], s[2], (0, 1), (low_taken_dve, g_taken_dve))
                elif s[0] == "X":
                    dve.wait_ge(low_moved, 16 * 5 * (s[1] + 1))
                    dve.wait_ge(g_taken_act, CHUNKS * (s[1] + 1))
                    nc.vector.tensor_copy(Xhi[:, :, :], X[:, :, :]).then_inc(x_hi_made, 1)
                    dve.wait_ge(x_hi_made, s[1] + 1)
                    nc.vector.tensor_tensor(Xlo[:, :, :], X[:, :, :], Xhi[:, :, :].bitcast(F32),
                                            ALU.subtract).then_inc(x_split, 1)
                elif s[0] == "A" and s[2] < 2:
                    h = z[:, BANK * s[3]:BANK * s[3] + BANK].rearrange("p (a b) -> p a b", b=P)
                    hi, lo = (x[s[2]][:, 4 * s[3]:4 * s[3] + 4, :] for x in (hhi, hlo))
                    for a in range(0, 4, 2):
                        dve.wait_ge(h_put, 2 * H_JOB[s] + 1 + a // 2)
                        nc.vector.tensor_copy(hi[:, a:a + 2], h[:, a:a + 2]).then_inc(h_hi_made, 1)
                    dve.wait_ge(h_hi_made, 2 * (S_JOB[s] + 1))
                    nc.vector.tensor_tensor(lo, h, hi.bitcast(F32), ALU.subtract).then_inc(h_split, 1)

        @block.scalar
        def _(act):
            act.dma_start(dn[:, :, :], dense.rearrange("(p k) f -> p k f", k=TILES)).then_inc(dense_loaded, 16)
            act.dma_start(vec[:, :], cols).then_inc(vec_loaded, 16)
            made = [0]

            def relu(dst, src, col):
                return nc.scalar.activation(dst, src, ACT.Relu, bias=vec[0:dst.shape[0], col:col + 1])

            def bottom(dst, src, col):
                made[0] += 1
                act.wait_ge(bottom_product, made[0])
                last = (nc.scalar.copy(dst, src) if col is None else relu(dst, src, col))
                last.then_inc(bottom_out, 1)

            for s in ORDER:
                if s[0] == "W":
                    layer, t = piece(s[1])
                    act.wait_ge(raw_loaded[s[1] % RAW], 16 * (s[1] // RAW + 1))
                    if layer == 2:
                        act.wait_ge(bottom_product, 8)
                    nc.scalar.copy(whi[layer][:, t, :], raw[:, s[1] % RAW, :]).then_inc(w_hi_made, 1)
                elif s[0] == "BT":
                    bottom(xT[:, :], psO[0][0:NUM_DENSE, :], None)
                    act.wait_ge(vec_loaded, 16)
                elif s[0] == "B0":
                    bottom(g1[:, s[1], :], psG[s[1] // 2][:, s[1] % 2, :], C_BB0 + s[1])
                elif s[0] == "B1":
                    bottom(g2[:, s[1], :], psO[s[1]][:, :], C_BB1 + s[1])
                elif s[0] == "B2":
                    bottom(D[:, :], psG[0][:, 0, :], C_BB2)
                elif s[0] == "F" and s[2] % 2 == 1:
                    put_features(nc.scalar.copy, act, s)
                elif s[0] == "G":
                    if s[2] == 0 and s[1] > 0:
                        act.wait_ge(x_split, s[1])
                    take_pairs(nc.scalar.copy, act, s[1], s[2], (2, 3), (low_taken_act, g_taken_act))
                elif s[0] == "M" and s[4] == PARTS[s[2]] - 1:
                    _, k, layer, half, _ = s
                    o_wait_full(act, s)
                    if layer == 2:
                        dst = z2[:, :]
                    else:
                        dst = z[:, BANK * half:BANK * half + BANK]
                        if (k, layer) == (0, 0):
                            act.wait_ge(w_lo_made, PIECES)
                        else:
                            before = (k, 0) if layer == 1 else (k - 1, 1)
                            act.wait_ge(h_split, S_JOB[("A", *before, half)] + 1)
                    nc.scalar.copy(dst, psO[O_JOB[s[:4]] % 2][:, :]).then_inc(z_put, 1)
                elif s[0] == "A":
                    _, k, layer, half = s
                    n = T_JOB[s]
                    t_wait_full(act, s)
                    dst = z2 if layer == 2 else z
                    col = (C_TB0, C_TB1, C_TB2)[layer] + 4 * half
                    for a in range(4):
                        at = BANK * half + P * a
                        last = relu(dst[:, at:at + P], psT[n % 2][:, P * a:P * a + P], col + a)
                        if a % 2:
                            last.then_inc(h_put, 1)
                elif s[0] == "M3":
                    n = T_JOB[s]
                    t_wait_full(act, s)
                    for m in range(2):
                        last = relu(h4[:, m, :], psT[n % 2][:, P * m:P * m + P], C_TB3 + m)
                    last.then_inc(h4_put, 1)
                elif s[0] == "M4":
                    n = T_JOB[s]
                    t_wait_full(act, s)
                    relu(out_row[0:1, s[1]:P * TILES:TILES], psT[n % 2][0:1, 0:P], C_TB4).then_inc(row_put, 1)


_LAYOUT = ["tables", "sparse", "dense", "cols", "bw0", "bw1", "bw2", "tw0", "tw1", "tw2", "tw3"]


def row_order():
    first, total = BOTTOM[-1], BOTTOM[-1] + 351
    pair = {}
    for i in range(27):
        for j in range(i + 1, 27):
            pair[i, j] = first + len(pair)
    order = np.full(4 * P, total)
    order[:first] = np.arange(first)

    def place(t, slot, i, j):
        order[P * (1 + t) + slot] = pair.pop((i, j))

    for q in range(4):
        for t in range(SETS_T):
            for i in range(HIGH + SETS_T * q + t):
                place(t, 32 * q + i, i, HIGH + SETS_T * q + t)
            for i in range(LOW_J[q] + t):
                place(t, 32 * q + 32 - LOW_ROWS[q] + i, i, LOW_J[q] + t)
    for t in range(2):
        for i in range(1 + t):
            place(t, LAST_SLOT + i, i, 1 + t)
    assert not pair
    return order


def kernel(**inputs):
    import concourse.bacc as _bacc
    from concourse.bass_utils import run_bass_kernel_spmd as _run

    a = {n.replace("L0_rec_", ""): np.ascontiguousarray(x) for n, x in inputs.items()}

    def by_partition(x):
        return x.reshape(-1, P).T

    cols = np.zeros((P, NCOLS), np.float32)
    for name, at in (("bb0", C_BB0), ("bb1", C_BB1), ("bb2", C_BB2), ("tb0", C_TB0), ("tb1", C_TB1), ("tb2", C_TB2),
                     ("tb3", C_TB3), ("tw4", C_TW4)):
        x = by_partition(a[name])
        cols[:, at:at + x.shape[1]] = x
    cols[0, C_TB4] = a["tb4"][0]
    tw0 = np.concatenate([a["tw0"], np.zeros((1, TOP[0]), np.float32)])[row_order()]
    given = {
        "tables": a["emb_tables"].reshape(NUM_SPARSE * VOCAB, DIM), "sparse": a["r_sparse"], "dense": a["r_dense"],
        "cols": cols, "bw0": a["bw0"], "bw1": a["bw1"], "bw2": a["bw2"], "tw0": tw0, "tw1": a["tw1"],
        "tw2": a["tw2"], "tw3": a["tw3"],
    }
    nc = _bacc.Bacc("TRN2", target_bir_lowering=False, num_devices=1)
    args = [nc.dram_tensor(f"in_{n}", given[n].shape, mybir.dt.from_np(given[n].dtype), kind="ExternalInput").ap()
            for n in _LAYOUT]
    out = nc.dram_tensor("out", (P * TILES,), F32, kind="ExternalOutput").ap()
    dlrm(nc, *args, out)
    r = _run(nc, [{f"in_{n}": given[n] for n in _LAYOUT}], core_ids=[0])
    return r.results[0]["out"]
```

```python
from contextlib import ExitStack

import numpy as np

import concourse.bass as bass
from concourse import mybir

P = 128
TILES = 4
NUM_SPARSE = 26
NUM_DENSE = 13
VOCAB = 12500
DIM = 128
BOTTOM = [512, 256, 128]
TOP = [1024, 1024, 512, 256, 1]
M3_N = TOP[3]
BANK = 512

F32 = mybir.dt.float32
F32R = mybir.dt.float32r
I32 = mybir.dt.int32
ALU = mybir.AluOpType
ACT = mybir.ActivationFunctionType

FEATURES = 1 + NUM_SPARSE
SLOTS = 32
HIGH = 15
SETS_T = 3
LOW_ROWS = [14, 11, 8, 5]
LOW_J = [12, 9, 6, 3]
LAST_SLOT, LAST_ROWS = 16, 2
NLOW = HIGH - 1

GROUPS = P // 4
GCHUNK = 8
CHUNKS = GROUPS // GCHUNK
GROWS = 3 * SLOTS + FEATURES
GCOLS = 4 * NUM_SPARSE

CUTS = [(0, 1, 2, 4), (0, 4, 6, 8), (0, 1, 4, 6, 8)]
RING = 18
RAW = 5
FJOB_TABLES = [0, 4, 8, 12, NLOW, 18, 22, NUM_SPARSE - 1, NUM_SPARSE]
FJOBS = len(FJOB_TABLES) - 1
LOW_JOBS = FJOB_TABLES.index(NLOW)
JOB_OF_TABLE = [j for j in range(FJOBS) for _ in range(FJOB_TABLES[j], FJOB_TABLES[j + 1])]

C_BB0, C_BB1, C_BB2, C_TB0, C_TB1, C_TB2, C_TB4, C_RAW, C_HI = 0, 4, 6, 7, 15, 23, 27, 28, 29
NCOLS = 30

PIECE_LAYER = [0] * 4 + [1] * 8 + [3] + [2] * 4
PIECES = len(PIECE_LAYER)
FIRST_PIECE = [PIECE_LAYER.index(layer) for layer in range(4)]


def stages():
    order = [("BT",), ("B0", 0), ("B0", 1), ("B0", 2), ("B0", 3), ("W", 0), ("W", 1), ("B1", 0), ("W", 2),
             ("W", 3), ("W", 4), ("F", 0, 0), ("F", 0, 1), ("B1", 1), ("W", 5), ("F", 0, 2), ("B2",), ("D", 0),
             ("F", 0, 3), ("W", 6), ("W", 7), ("GL", 0, 0), ("DS",), ("GL", 0, 1), ("W", 8), ("W", 9),
             ("F", 0, 4), ("GL", 0, 2), ("GL", 0, 3), ("F", 0, 5), ("F", 0, 6), ("F", 0, 7), ("W", 10),
             ("M", 0, 0, 0, 0), ("GH", 0, 0), ("GH", 0, 1), ("W", 11), ("GH", 0, 2), ("GH", 0, 3), ("X", 0),
             ("W", 12), ("F", 1, 0), ("W", 13), ("F", 1, 1), ("W", 14)]
    for k in range(TILES):
        m00, m01, m10, m11, m2 = ([("M", k, layer, n, part) for part in range(len(CUTS[layer]) - 1)]
                                  for layer, n in ((0, 0), (0, 1), (1, 0), (1, 1), (2, 0)))
        a0, a1 = ([("A", k, layer, half) for half in range(2)] for layer in range(2))
        f = [("F", k + 1, j) for j in range(FJOBS)] + [("D", k + 1)]
        g = [("G", k + 1, c) for c in range(CHUNKS)]
        x = ("X", k + 1)
        a2, m3 = ("A", k - 1, 2, 0), ("M3", k - 1)
        last = [("M", k, 2, 1, part) for part in range(len(CUTS[2]) - 1)]
        if k == 0:
            order += [m01[0], m00[1], m00[2], m01[1], a0[0], m01[2], f[2], a0[1], ("W", 15), ("W", 16), m10[0],
                      f[3], m10[1], m10[2], f[4], m11[0], a1[0], f[5], m11[1], f[6], f[7], f[8], m11[2], g[0],
                      g[1], a1[1], g[2], g[3], m2[0], m2[1], m2[2], x, m2[3]]
        elif k + 1 < TILES:
            order += [m00[0], f[0], a2, m00[1], m00[2], m01[0], m01[1], a0[0], f[1], m01[2], f[2], m3, a0[1],
                      m10[0], f[3], m10[1], m10[2], f[4], f[5], m11[0], f[6], f[7], f[8], m11[1], g[0], g[1],
                      a1[0], m11[2], g[2], g[3], a1[1], m2[0], m2[1], m2[2], m2[3], x]
        else:
            order += [m00[0], a2, m01[0], m00[1], m00[2], m01[1], m01[2], a0[0], m3, a0[1], m10[0], m10[1],
                      m10[2], m11[0], a1[0], m11[1], m11[2], m2[0], m2[1], a1[1], last[0], last[1], m2[2], m2[3],
                      last[2], last[3], ("A", k, 2, 0), ("A", k, 2, 1), ("M3", k)]
    return order


ORDER = stages()
T_KINDS = ("F", "A", "M3")
T_JOB = {s: n for n, s in enumerate(s for s in ORDER if s[0] in T_KINDS)}
O_JOB = {s[:4]: n for n, s in enumerate(s for s in ORDER if s[0] == "M" and s[4] == 0)}


def columns(s):
    width = BANK // 2 if s[1:3] == (TILES - 1, 2) else BANK
    return slice(width * s[3], width * (s[3] + 1))


A_PAIRS, pairs = {}, 0
for stage in ORDER:
    if stage[0] == "A":
        pairs += 2 if columns(stage).stop - columns(stage).start == BANK else 1
        A_PAIRS[stage] = pairs
T_STAGE = {n: s for s, n in T_JOB.items()}
G_JOB = {s: n for n, s in enumerate(s for s in ORDER if s[0] in ("G", "GL", "GH"))}
G_STAGE = {n: s for s, n in G_JOB.items()}


def f_put(s):
    n = T_JOB[s]
    return n % 2, sum(T_STAGE[m][0] == "F" for m in range(n % 2, n + 1, 2))


def in_features(j):
    return range(FJOB_TABLES[j], FJOB_TABLES[j + 1])


def dlrm(nc, tables, sparse, dense, cols, bw0, bw1, bw2, tw0, tw1, tw2, tw3, last_rows, out):
    with ExitStack() as ctx:
        def sb(name, shape, dt, where=None):
            return (where or ctx).enter_context(nc.sbuf_tensor(name, shape, dt))

        def sem(name):
            return ctx.enter_context(nc.semaphore(name))

        ident = sb("ident", [P, P], F32)
        vec = sb("vec", [P, NCOLS], F32)
        rows = sb("rows", [P, TILES * NUM_SPARSE], I32)
        wide = sb("wide", [P, 2, M3_N], F32)
        y = sb("y", [P, 2, TILES], F32)
        h2hi = sb("h2hi", [P, 4, P], F32R)
        h2lo = sb("h2lo", [P, 4, P], F32R)
        emb = sb("emb", [P, RING, DIM], F32)
        FT = sb("FT", [P, P, SLOTS], F32)
        D = sb("D", [P, BANK], F32)
        Dhi = sb("Dhi", [P, BANK], F32R)
        Dlo = sb("Dlo", [P, BANK], F32R)
        X = sb("X", [P, SETS_T, P], F32)
        Xhi = sb("Xhi", [P, SETS_T, P], F32R)
        Xlo = sb("Xlo", [P, SETS_T, P], F32R)
        low = sb("low", [NLOW, NLOW, P], F32)
        z2 = sb("z2", [P, BANK], F32)
        with ExitStack() as early:
            raw = sb("raw", [P, RAW, 1024], F32, early)
        hhi1 = sb("hhi1", [P, 8, P], F32R)
        hlo1 = sb("hlo1", [P, 8, P], F32R)
        z = sb("z", [P, 1024], F32)
        hhi = [sb("hhi0", [P, 8, P], F32R), hhi1]
        hlo = [sb("hlo0", [P, 8, P], F32R), hlo1]
        hhi.append(h2hi)
        hlo.append(h2lo)
        whi = [sb(f"whi{n}", [P, 4 * (1, 2)[n], 1024], F32R) for n in range(2)]
        wlo = [sb(f"wlo{n}", [P, 4 * (1, 2)[n], 1024], F32R) for n in range(2)]
        with ExitStack() as early:
            sp_idx = sb("sp_idx", [P, TILES * NUM_SPARSE], I32, early)
            base = sb("base", [P, TILES * NUM_SPARSE], I32, early)
            wrap = sb("wrap", [P, TILES * NUM_SPARSE], F32, early)
            dn = sb("dn", [P, TILES, NUM_DENSE], F32, early)
            dn_hi = sb("dn_hi", [P, TILES, NUM_DENSE], F32R, early)
            dn3 = sb("dn3", [P, TILES, 3, NUM_DENSE], F32, early)
            xT = sb("xT", [3 * NUM_DENSE, BANK], F32R, early)
            b0 = sb("b0", [3 * NUM_DENSE, BOTTOM[0]], F32, early)
            b0_hi = sb("b0_hi", [3 * NUM_DENSE, BOTTOM[0]], F32R, early)
            b0_parts = sb("b0_parts", [3 * NUM_DENSE, BOTTOM[0]], F32R, early)
            b1 = sb("b1", [P, 4, BOTTOM[1]], F32, early)
            b2 = sb("b2", [P, 2, BOTTOM[2]], F32, early)
            g1 = sb("g1", [P, 4, BANK], F32, early)
            g2 = sb("g2", [P, 2, BANK], F32, early)
        whi.append(sb("whi2", [P, 4, 1024], F32R))
        wlo.append(sb("wlo2", [P, 4, 1024], F32R))
        whi.append(sb("whi3", [P, 1, 1024], F32R))
        wlo.append(sb("wlo3", [P, 1, 1024], F32R))

        psT = [ctx.enter_context(nc.psum_tensor(f"psT{n}", [P, BANK], F32)) for n in range(2)]
        psG = [ctx.enter_context(nc.psum_tensor(f"psG{n}", [P, 2, BANK], F32)) for n in range(2)]
        psO = [ctx.enter_context(nc.psum_tensor(f"psO{n}", [P, BANK], F32)) for n in range(2)]

        idx_loaded = sem("idx_loaded")
        dense_loaded = sem("dense_loaded")
        vec_loaded = sem("vec_loaded")
        bw_loaded = [sem(f"bw{n}_loaded") for n in range(3)]
        wide_loaded = sem("wide_loaded")
        raw_loaded = [sem(f"raw{n}_loaded") for n in range(RAW)]
        base_made = sem("base_made")
        ident_made = sem("ident_made")
        idx_step = sem("idx_step")
        pads_zero = sem("pads_zero")
        gathered = [sem(f"gathered{n}") for n in range(RING)]
        w_hi_made = sem("w_hi_made")
        w_lo_made = sem("w_lo_made")
        dense_step = sem("dense_step")
        b0_step = sem("b0_step")
        bottom_product = sem("bottom_product")
        bottom_out = sem("bottom_out")
        d_hi_made = sem("d_hi_made")
        d_split = sem("d_split")
        t_full = [sem(f"t_full{n}") for n in range(2)]
        t_put = [sem(f"t_put{n}") for n in range(2)]
        ft0_put = sem("ft0_put")
        g_full = sem("g_full")
        low_taken_dve = sem("low_taken_dve")
        low_taken_act = sem("low_taken_act")
        g_taken_dve = sem("g_taken_dve")
        g_taken_act = sem("g_taken_act")
        low_moved = sem("low_moved")
        x_hi_made = sem("x_hi_made")
        x_split = sem("x_split")
        o_full = [sem(f"o_full{n}") for n in range(2)]
        z_put = sem("z_put")
        h_put = sem("h_put")
        h_hi_made = sem("h_hi_made")
        h_split = sem("h_split")
        h4_put = sem("h4_put")
        dot_made = sem("dot_made")
        y_put = sem("y_put")
        stored = sem("stored")

        w_src = [
            tw0.rearrange("(t p) n -> p t n", p=P),
            tw1.rearrange("(t p) n -> p t n", p=P),
            tw2.rearrange("(u v p) n -> p u v n", p=P, v=2),
            tw3.rearrange("(u v p) n -> p u v n", p=P, v=4),
        ]

        def piece(p):
            layer = PIECE_LAYER[p]
            return layer, p - FIRST_PIECE[layer]

        def pieces_read(*slots):
            return 1 + max(p for p in range(PIECES) if p % RAW in slots)

        def t_wait_full(eng, s):
            n = T_JOB[s]
            eng.wait_ge(t_full[n % 2], n // 2 + 1)

        def o_wait_full(eng, s):
            n = O_JOB[s[:4]]
            eng.wait_ge(o_full[n % 2], n // 2 + 1)

        block = ctx.enter_context(nc.Block())

        @block.sync
        def _(sp):
            def move_low(k):
                sp.wait_ge(low_taken_dve, CHUNKS * (k + 1))
                sp.wait_ge(low_taken_act, CHUNKS * (k + 1))
                for q in range(4):
                    r = LOW_ROWS[q]
                    sp.dma_start(X[32 * q + 32 - r:32 * q + 32, :, :],
                                 low[0:r, LOW_J[q] - 1:LOW_J[q] - 1 + SETS_T, :]).then_inc(low_moved, 16)
                sp.dma_start(X[LAST_SLOT:LAST_SLOT + LAST_ROWS, 0:2, :],
                             low[0:LAST_ROWS, 0:2, :]).then_inc(low_moved, 16)

            sp.dma_start(sp_idx[:, :], sparse.rearrange("(p k) f -> p (k f)", k=TILES)).then_inc(idx_loaded, 16)
            for n in range(3):
                sp.dma_start(b0[NUM_DENSE * n:NUM_DENSE * (n + 1), :], bw0).then_inc(bw_loaded[0], 16)
            sp.dma_start(b1[:, :, :], bw1.rearrange("(t p) n -> p t n", p=P)).then_inc(bw_loaded[1], 16)
            sp.dma_start(b2[:, :, :], bw2.rearrange("(t p) n -> p t n", p=P)).then_inc(bw_loaded[2], 16)
            for p in range(PIECES):
                if p >= RAW:
                    sp.wait_ge(w_lo_made, p - RAW + 1)
                layer, t = piece(p)
                if p == FIRST_PIECE[3]:
                    n = NUM_SPARSE - 3
                    sp.wait_ge(gathered[n % RING], 16 * (n // RING + 1))
                elif p == FIRST_PIECE[2] + 1:
                    move_low(0)
                dst = raw[:, p % RAW, :]
                if layer >= 2:
                    dst = dst.rearrange("p (v n) -> p v n", n=TOP[layer])
                sp.dma_start(dst, w_src[layer][:, t]).then_inc(raw_loaded[p % RAW], 16)
            sp.dma_start(wide[:, :, :], last_rows.partition_broadcast(P)).then_inc(wide_loaded, 16)
            for k in range(1, TILES):
                move_low(k)
            sp.wait_ge(y_put, 1)
            sp.dma_start(out.rearrange("(p k) -> p k", k=TILES), y[:, 1, :]).then_inc(stored, 16)
            sp.wait_ge(stored, 16)

        @block.gpsimd
        def _(pool):
            nc.gpsimd.iota(base[:, :], pattern=[[0, TILES], [VOCAB, NUM_SPARSE]], base=0,
                           channel_multiplier=0).then_inc(base_made, 1)
            nc.gpsimd.memset(ident[:, :], 0.0).then_inc(ident_made, 1)
            pool.wait_ge(ident_made, 1)
            nc.gpsimd.affine_select(out=ident[:, :], in_=ident[:, :], compare_op=ALU.not_equal, fill=1.0, base=0,
                                    pattern=[[-1, P]], channel_multiplier=1).then_inc(ident_made, 1)
            pool.wait_ge(idx_step, 3)
            for n in range(TILES * NUM_SPARSE):
                if n >= RING:
                    k, f = divmod(n - RING, NUM_SPARSE)
                    t_wait_full(pool, ("F", k, JOB_OF_TABLE[f]))
                nc.gpsimd.indirect_dma_start(
                    out=emb[:, n % RING, :], out_offset=None, in_=tables,
                    in_offset=bass.IndirectOffsetOnAxis(ap=rows[:, n:n + 1], axis=0),
                ).then_inc(gathered[n % RING], 16)

        @block.tensor
        def _(pe):
            def t_bank(s):
                n = T_JOB[s]
                if n >= 2:
                    before = T_STAGE[n - 2]
                    if before[0] == "F":
                        bank, count = f_put(before)
                        pe.wait_ge(t_put[bank], count)
                    elif before[0] == "A":
                        pe.wait_ge(h_put, A_PAIRS[before])
                    else:
                        pe.wait_ge(dot_made, before[1] + 1)
                return psT[n % 2], t_full[n % 2]

            def features(s):
                ps, full = t_bank(s)
                for a, f in enumerate(in_features(s[2])):
                    n = s[1] * NUM_SPARSE + f
                    pe.wait_ge(gathered[n % RING], 16 * (n // RING + 1))
                    last = nc.tensor.transpose(ps[:, P * a:P * a + P], emb[:, n % RING, :], ident[:, :])
                last.then_inc(full, 1)

            def gram(s):
                kind, k, c = s
                m = G_JOB[s]
                if c == 0:
                    jobs = range(LOW_JOBS if kind == "GL" else FJOBS)
                    for bank, count in sorted(dict(f_put(("F", k, j)) for j in jobs).items()):
                        pe.wait_ge(t_put[bank], count)
                    pe.wait_ge(ft0_put, k + 1)
                    pe.wait_ge(pads_zero, 1)
                if m >= 2:
                    kind2, k2, c2 = G_STAGE[m - 2]
                    dve_taken, act_taken = ((low_taken_dve, low_taken_act) if kind2 == "GL" else
                                            (g_taken_dve, g_taken_act))
                    pe.wait_ge(dve_taken, CHUNKS * k2 + c2 + 1)
                    pe.wait_ge(act_taken, CHUNKS * k2 + c2 + 1)
                for g in range(GCHUNK):
                    b = 4 * (GCHUNK * c + g)
                    last = nc.tensor.matmul(psG[m % 2][0:GROWS, g // 4, GCOLS * (g % 4):GCOLS * (g % 4) + GCOLS],
                                            FT[:, b:b + 4, :].rearrange("p b f -> p (b f)")[:, 0:GROWS],
                                            FT[:, b:b + 4, 1:1 + NUM_SPARSE], start=True, stop=True)
                last.then_inc(g_full, 1)

            def product(s):
                _, k, layer, n, part = s
                j = O_JOB[s[:4]]
                if j >= 2 and part == 0:
                    pe.wait_ge(z_put, j - 1)
                kt = CUTS[layer][-1]
                for t in range(CUTS[layer][part], CUTS[layer][part + 1]):
                    if layer == 0:
                        hi, lo = ((Dhi[:, P * k:P * k + P], Dlo[:, P * k:P * k + P]) if t == 0 else
                                  (Xhi[:, t - 1, :], Xlo[:, t - 1, :]))
                        pe.wait_ge(*((d_split, 1) if t == 0 else (x_split, SETS_T * k + t)))
                    else:
                        hi, lo = hhi[layer - 1][:, t, :], hlo[layer - 1][:, t, :]
                        if t % 2 == 0:
                            pe.wait_ge(h_split, A_PAIRS["A", k, layer - 1, t // 4] - 1 + t % 4 // 2)
                    if layer < 2:
                        w = [x[layer][:, t, BANK * n:BANK * n + BANK] for x in (whi, wlo)]
                        pe.wait_ge(w_lo_made, FIRST_PIECE[layer] + t + 1)
                    else:
                        at = columns(s)
                        w = [x[2][:, t // 2, BANK * (t % 2) + at.start:BANK * (t % 2) + at.stop] for x in (whi, wlo)]
                        pe.wait_ge(w_lo_made, FIRST_PIECE[2] + t // 2 + 1)
                    for i, (a, b) in enumerate(((hi, w[0]), (hi, w[1]), (lo, w[0]))):
                        width = columns(s).stop - columns(s).start
                        last = nc.tensor.matmul(psO[j % 2][:, 0:width], a, b, start=(t == 0 and i == 0),
                                                stop=(t == kt - 1 and i == 2))
                if t == kt - 1:
                    last.then_inc(o_full[j % 2], 1)

            def turn(s):
                _, k, layer, half = s
                pe.wait_ge(z_put, O_JOB["M", k, layer, half] + 1)
                ps, full = t_bank(s)
                src = z2 if layer == 2 else z
                for a, at in enumerate(range(columns(s).start, columns(s).stop, P)):
                    last = nc.tensor.transpose(ps[:, P * a:P * a + P], src[:, at:at + P], ident[:, :])
                last.then_inc(full, 1)

            for s in ORDER:
                if s[0] == "BT":
                    pe.wait_ge(ident_made, 2)
                    pe.wait_ge(dense_step, 3)
                    for k in range(TILES):
                        last = nc.tensor.transpose(psO[0][0:3 * NUM_DENSE, P * k:P * k + P],
                                                   dn3[:, k, :, :].rearrange("p n f -> p (n f)"), ident[:, :])
                    last.then_inc(bottom_product, 1)
                elif s[0] == "B0":
                    pe.wait_ge(bottom_out, 1)
                    pe.wait_ge(b0_step, 3)
                    nc.tensor.matmul(psG[s[1] // 2][:, s[1] % 2, :], b0_parts[:, P * s[1]:P * s[1] + P], xT[:, :],
                                     start=True, stop=True).then_inc(bottom_product, 1)
                elif s[0] == "B1":
                    pe.wait_ge(bw_loaded[1], 16)
                    for t in range(4):
                        pe.wait_ge(bottom_out, 2 + t)
                        last = nc.tensor.matmul(psO[s[1]][:, :], b1[:, t, P * s[1]:P * s[1] + P], g1[:, t, :],
                                                start=(t == 0), stop=(t == 3))
                    last.then_inc(bottom_product, 1)
                elif s[0] == "B2":
                    pe.wait_ge(bw_loaded[2], 16)
                    for t in range(2):
                        pe.wait_ge(bottom_out, 6 + t)
                        last = nc.tensor.matmul(psG[0][:, 0, :], b2[:, t, :], g2[:, t, :],
                                                start=(t == 0), stop=(t == 1))
                    last.then_inc(bottom_product, 1)
                elif s[0] == "F":
                    features(s)
                elif s in G_JOB:
                    gram(s)
                elif s[0] == "M":
                    product(s)
                elif s[0] == "A":
                    turn(s)
                elif s[0] == "M3":
                    ps, full = t_bank(s)
                    pe.wait_ge(w_lo_made, FIRST_PIECE[3] + 1)
                    for t in range(4):
                        if t % 2 == 0:
                            first_pair = A_PAIRS["A", s[1], 2, 0] - (0 if s[1] == TILES - 1 else 1)
                            pe.wait_ge(h_split, first_pair + t // 2)
                        for i, (a, b) in enumerate(((h2hi, whi[3]), (h2hi, wlo[3]), (h2lo, whi[3]))):
                            last = nc.tensor.matmul(ps[:, 0:M3_N], a[:, t, :], b[:, 0, M3_N * t:M3_N * (t + 1)],
                                                    start=(t == 0 and i == 0), stop=(t == 3 and i == 2))
                    last.then_inc(full, 1)

        def put_features(copy, eng, s):
            t_wait_full(eng, s)
            n = T_JOB[s]
            fs = in_features(s[2])
            return copy(FT[:, :, 1 + fs[0]:1 + fs[0] + len(fs)],
                        psT[n % 2][:, 0:P * len(fs)].rearrange("p (f b) -> p b f", f=len(fs))).then_inc(t_put[n % 2], 1)

        def take_pairs(copy, eng, s, batches, low_taken, g_taken):
            kind, k, c = s
            m = G_JOB[s]
            eng.wait_ge(g_full, m + 1)

            def pairs(b):
                return psG[m % 2][:, :, 0:4 * GCOLS].rearrange("p u (g c j) -> p j u g c", g=4, c=4)[:, :, :, :, b]

            def at(dst, b):
                return dst[:, :, 4 * GCHUNK * c + b:4 * GCHUNK * (c + 1):4].rearrange("p j (u g) -> p j u g", u=2)

            if kind != "GH":
                for b in batches:
                    last = copy(at(low, b), pairs(b)[32 * b:32 * b + NLOW, 0:NLOW])
                last.then_inc(low_taken, 1)
            if kind != "GL":
                for b in batches:
                    for q in range(4):
                        for t0, t1, r in (((0, 2, LAST_SLOT), (2, 3, LAST_SLOT + LAST_ROWS)) if q == 0 else
                                          ((0, SETS_T, SLOTS - LOW_ROWS[q]),)):
                            j = HIGH - 1 + SETS_T * q
                            last = copy(at(X[32 * q:32 * q + r, t0:t1], b),
                                        pairs(b)[32 * b:32 * b + r, j + t0:j + t1])
                last.then_inc(g_taken, 1)

        @block.vector
        def _(dve):
            dve.wait_ge(idx_loaded, 16)
            nc.vector.tensor_scalar(wrap[:, :], sp_idx[:, :], 0.0, float(VOCAB), ALU.is_lt,
                                    ALU.mult).then_inc(idx_step, 1)
            dve.wait_ge(idx_step, 1)
            nc.vector.scalar_tensor_tensor(out=wrap[:, :], in0=sp_idx[:, :], scalar=float(-VOCAB), in1=wrap[:, :],
                                           op0=ALU.max, op1=ALU.add).then_inc(idx_step, 1)
            dve.wait_ge(idx_step, 2)
            dve.wait_ge(base_made, 1)
            nc.vector.scalar_tensor_tensor(out=rows[:, :], in0=wrap[:, :], scalar=float(VOCAB - 1), in1=base[:, :],
                                           op0=ALU.min, op1=ALU.add).then_inc(idx_step, 1)

            dve.wait_ge(dense_loaded, 16)
            nc.vector.tensor_copy(dn_hi[:, :, :], dn[:, :, :]).then_inc(dense_step, 1)
            dve.wait_ge(dense_step, 1)
            nc.vector.tensor_tensor(dn3[:, :, 1, :], dn[:, :, :], dn_hi[:, :, :].bitcast(F32),
                                    ALU.subtract).then_inc(dense_step, 1)
            nc.vector.tensor_copy(dn3[:, :, 0:3:2, :], dn_hi[:, :, :].bitcast(F32).unsqueeze(2).broadcast_to(
                [P, TILES, 2, NUM_DENSE])).then_inc(dense_step, 1)
            dve.wait_ge(bw_loaded[0], 48)
            dve.wait_ge(vec_loaded, 16)
            nc.vector.tensor_copy(b0_hi[:, :], b0[:, :]).then_inc(b0_step, 1)
            nc.vector.tensor_scalar(b0[:, :], b0[:, :], vec[0:3 * NUM_DENSE, C_RAW:C_RAW + 1], None,
                                    ALU.mult).then_inc(b0_step, 1)
            dve.wait_ge(b0_step, 2)
            nc.vector.scalar_tensor_tensor(out=b0_parts[:, :], in0=b0_hi[:, :].bitcast(F32),
                                           scalar=vec[0:3 * NUM_DENSE, C_HI:C_HI + 1], in1=b0[:, :],
                                           op0=ALU.mult, op1=ALU.add).then_inc(b0_step, 1)
            nc.vector.memset(FT[:, :, HIGH:SLOTS], 0.0).then_inc(pads_zero, 1)

            for s in ORDER:
                if s[0] == "W":
                    layer, t = piece(s[1])
                    dve.wait_ge(w_hi_made, s[1] + 1)
                    if layer == 2:
                        dve.wait_ge(bottom_product, 8)
                    nc.vector.tensor_tensor(wlo[layer][:, t, :], raw[:, s[1] % RAW, :],
                                            whi[layer][:, t, :].bitcast(F32), ALU.subtract).then_inc(w_lo_made, 1)
                elif s[0] == "DS":
                    nc.vector.tensor_copy(Dhi[:, :], D[:, :]).then_inc(d_hi_made, 1)
                    dve.wait_ge(d_hi_made, 1)
                    nc.vector.tensor_tensor(Dlo[:, :], D[:, :], Dhi[:, :].bitcast(F32),
                                            ALU.subtract).then_inc(d_split, 1)
                elif s[0] == "F":
                    if s[1:] == (0, 4):
                        dve.wait_ge(g_full, CHUNKS)
                    if s[2] % 2 == 0:
                        put_features(nc.vector.tensor_copy, dve, s)
                elif s[0] == "D":
                    if s[1] == 0:
                        dve.wait_ge(bottom_out, 8)
                    nc.vector.tensor_copy(FT[:, :, 0], D[:, P * s[1]:P * s[1] + P]).then_inc(ft0_put, 1)
                elif s in G_JOB:
                    take_pairs(nc.vector.tensor_copy, dve, s, (0, 1), low_taken_dve, g_taken_dve)
                elif s[0] == "X":
                    dve.wait_ge(low_moved, 16 * 5 * (s[1] + 1))
                    dve.wait_ge(g_taken_dve, CHUNKS * (s[1] + 1))
                    dve.wait_ge(g_taken_act, CHUNKS * (s[1] + 1))
                    for t in range(SETS_T):
                        nc.vector.tensor_copy(Xhi[:, t], X[:, t]).then_inc(x_hi_made, 1)
                        dve.wait_ge(x_hi_made, SETS_T * s[1] + t + 1)
                        nc.vector.tensor_tensor(Xlo[:, t], X[:, t], Xhi[:, t].bitcast(F32),
                                                ALU.subtract).then_inc(x_split, 1)
                elif s[0] == "M3":
                    _, k = s
                    if k == 0:
                        dve.wait_ge(wide_loaded, 16)
                    t_wait_full(dve, s)
                    h4 = psT[T_JOB[s] % 2][:, 0:M3_N]
                    nc.vector.tensor_tensor(h4, h4, wide[:, 0, :], ALU.add).then_inc(h4_put, 1)
                    dve.wait_ge(h4_put, k + 1)
                    nc.vector.scalar_tensor_tensor(out=h4, in0=h4, scalar=0.0, in1=wide[:, 1, :],
                                                   op0=ALU.max, op1=ALU.mult,
                                                   accum_out=y[:, 0, k:k + 1]).then_inc(dot_made, 1)
                    if k == TILES - 1:
                        dve.wait_ge(vec_loaded, 16)
                        dve.wait_ge(dot_made, TILES)
                        nc.vector.tensor_scalar(y[:, 1, :], y[:, 0, :], vec[:, C_TB4:C_TB4 + 1], 0.0, ALU.add,
                                                ALU.max).then_inc(y_put, 1)
                elif s[0] == "A":
                    at = columns(s)
                    first, n = at.start // P, (at.stop - at.start) // P
                    h = (z2 if s[2] == 2 else z)[:, at].rearrange("p (a b) -> p a b", b=P)
                    hi, lo = (x[s[2]][:, first:first + n, :] for x in (hhi, hlo))
                    if s[2] == 2 and s[1] > 0:
                        t_wait_full(dve, ("M3", s[1] - 1))
                    if s[2] < 2 and s[1] == 0:
                        dve.wait_ge(w_lo_made, pieces_read(3, 4) if s[2] == 0 else pieces_read(0, 1))
                    for a in range(0, n, 2):
                        count = A_PAIRS[s] - (n - a) // 2 + 1
                        dve.wait_ge(h_put, count)
                        nc.vector.tensor_copy(hi[:, a:a + 2], h[:, a:a + 2]).then_inc(h_hi_made, 1)
                        dve.wait_ge(h_hi_made, count)
                        nc.vector.tensor_tensor(lo[:, a:a + 2], h[:, a:a + 2], hi[:, a:a + 2].bitcast(F32),
                                                ALU.subtract).then_inc(h_split, 1)

        @block.scalar
        def _(act):
            act.dma_start(dn[:, :, :], dense.rearrange("(p k) f -> p k f", k=TILES)).then_inc(dense_loaded, 16)
            act.dma_start(vec[:, :], cols).then_inc(vec_loaded, 16)
            made = [0]

            def relu(dst, src, col):
                return nc.scalar.activation(dst, src, ACT.Relu, bias=vec[0:dst.shape[0], col:col + 1])

            def bottom(dst, src, col):
                made[0] += 1
                act.wait_ge(bottom_product, made[0])
                last = (nc.scalar.copy(dst, src) if col is None else relu(dst, src, col))
                last.then_inc(bottom_out, 1)

            for s in ORDER:
                if s[0] == "W":
                    layer, t = piece(s[1])
                    act.wait_ge(raw_loaded[s[1] % RAW], 16 * (s[1] // RAW + 1))
                    if layer == 2:
                        act.wait_ge(bottom_product, 8)
                    nc.scalar.copy(whi[layer][:, t, :], raw[:, s[1] % RAW, :]).then_inc(w_hi_made, 1)
                elif s[0] == "BT":
                    bottom(xT[:, :], psO[0][0:3 * NUM_DENSE, :], None)
                    act.wait_ge(vec_loaded, 16)
                elif s[0] == "B0":
                    bottom(g1[:, s[1], :], psG[s[1] // 2][:, s[1] % 2, :], C_BB0 + s[1])
                elif s[0] == "B1":
                    bottom(g2[:, s[1], :], psO[s[1]][:, :], C_BB1 + s[1])
                elif s[0] == "B2":
                    bottom(D[:, :], psG[0][:, 0, :], C_BB2)
                elif s[0] == "F" and s[2] % 2 == 1:
                    if s[1:] == (0, 5):
                        act.wait_ge(g_full, CHUNKS)
                    put_features(nc.scalar.copy, act, s)
                elif s in G_JOB:
                    if s[2] == 0 and s[1] > 0:
                        act.wait_ge(x_split, SETS_T * s[1])
                    take_pairs(nc.scalar.copy, act, s, (2, 3), low_taken_act, g_taken_act)
                elif s[0] == "M" and s[4] == len(CUTS[s[2]]) - 2:
                    _, k, layer, half, _ = s
                    o_wait_full(act, s)
                    if layer == 2:
                        dst = z2[:, columns(s)]
                        if k > 0:
                            act.wait_ge(h_split, A_PAIRS["A", k - 1, 2, 0])
                    else:
                        dst = z[:, BANK * half:BANK * half + BANK]
                        if (k, layer) == (0, 0):
                            act.wait_ge(w_lo_made, pieces_read(2))
                        else:
                            before = (k, 0) if layer == 1 else (k - 1, 1)
                            act.wait_ge(h_split, A_PAIRS[("A", *before, half)])
                    width = columns(s).stop - columns(s).start
                    nc.scalar.copy(dst, psO[O_JOB[s[:4]] % 2][:, 0:width]).then_inc(z_put, 1)
                elif s[0] == "A":
                    _, k, layer, half = s
                    n = T_JOB[s]
                    t_wait_full(act, s)
                    dst = z2 if layer == 2 else z
                    col = (C_TB0, C_TB1, C_TB2)[layer] + columns(s).start // P
                    for a, at in enumerate(range(columns(s).start, columns(s).stop, P)):
                        last = relu(dst[:, at:at + P], psT[n % 2][:, P * a:P * a + P], col + a)
                        if a % 2:
                            last.then_inc(h_put, 1)


_LAYOUT = ["tables", "sparse", "dense", "cols", "bw0", "bw1", "bw2", "tw0", "tw1", "tw2", "tw3",
           "last_rows"]


def row_order():
    first, total = BOTTOM[-1], BOTTOM[-1] + 351
    pair = {}
    for i in range(27):
        for j in range(i + 1, 27):
            pair[i, j] = first + len(pair)
    order = np.full(4 * P, total)
    order[:first] = np.arange(first)

    def place(t, slot, i, j):
        order[P * (1 + t) + slot] = pair.pop((i, j))

    for q in range(4):
        for t in range(SETS_T):
            for i in range(HIGH + SETS_T * q + t):
                place(t, 32 * q + i, i, HIGH + SETS_T * q + t)
            for i in range(LOW_J[q] + t):
                place(t, 32 * q + 32 - LOW_ROWS[q] + i, i, LOW_J[q] + t)
    for t in range(2):
        for i in range(1 + t):
            place(t, LAST_SLOT + i, i, 1 + t)
    assert not pair
    return order


def kernel(**inputs):
    import concourse.bacc as _bacc
    from concourse.bass_utils import run_bass_kernel_spmd as _run

    a = {n.replace("L0_rec_", ""): np.ascontiguousarray(x) for n, x in inputs.items()}

    def by_partition(x):
        return x.reshape(-1, P).T

    cols = np.zeros((P, NCOLS), np.float32)
    for name, at in (("bb0", C_BB0), ("bb1", C_BB1), ("bb2", C_BB2), ("tb0", C_TB0), ("tb1", C_TB1), ("tb2", C_TB2)):
        x = by_partition(a[name])
        cols[:, at:at + x.shape[1]] = x
    cols[:, C_TB4] = a["tb4"][0]
    cols[2 * NUM_DENSE:3 * NUM_DENSE, C_RAW] = 1
    cols[0:3 * NUM_DENSE, C_HI] = 1 - 2 * cols[0:3 * NUM_DENSE, C_RAW]
    tw0 = np.concatenate([a["tw0"], np.zeros((1, TOP[0]), np.float32)])[row_order()]
    given = {
        "tables": a["emb_tables"].reshape(NUM_SPARSE * VOCAB, DIM), "sparse": a["r_sparse"], "dense": a["r_dense"],
        "cols": cols, "bw0": a["bw0"], "bw1": a["bw1"], "bw2": a["bw2"], "tw0": tw0, "tw1": a["tw1"],
        "tw2": a["tw2"], "tw3": a["tw3"], "last_rows": np.stack([a["tb3"], a["tw4"].reshape(-1)]),
    }
    nc = _bacc.Bacc("TRN2", target_bir_lowering=False, num_devices=1)
    args = [nc.dram_tensor(f"in_{n}", given[n].shape, mybir.dt.from_np(given[n].dtype), kind="ExternalInput").ap()
            for n in _LAYOUT]
    out = nc.dram_tensor("out", (P * TILES,), F32, kind="ExternalOutput").ap()
    dlrm(nc, *args, out)
    r = _run(nc, [{f"in_{n}": given[n] for n in _LAYOUT}], core_ids=[0])
    return r.results[0]["out"]
```
